# Optimizing a Trainium2 kernel written in Bass

```python
import numpy as np
import jax
import jax.numpy as jnp

def _softmax(x, axis=-1):
    return jax.nn.softmax(x, axis=axis)

def _gelu(x):
    return jax.nn.gelu(x, approximate=True)

def _silu(x):
    return jax.nn.silu(x)

def _sigmoid(x):
    return jax.nn.sigmoid(x)

def _layernorm(x, axis=-1, eps=1e-05):
    m = jnp.mean(x, axis=axis, keepdims=True)
    v = jnp.var(x, axis=axis, keepdims=True)
    return (x - m) / jnp.sqrt(v + eps)

def _scatter_add(tgt, idx, src, axis=0):
    return tgt.at[idx].add(src)

def _segment_sum(src, seg, n):
    return jax.ops.segment_sum(src, seg, n)
kernel_name = 'mk_recurrent_d1_jaxref_r8_f9bd36'

def setup_inputs(seed: int=0):
    np.random.seed(seed)
    _w = jnp.asarray

    def _L0_attn_setup():
        import jax, jax.numpy as jnp
        import numpy as np
        DIM = 128
        HEADS = 16
        DIM_HEAD = 64
        NUM_FREQS = 16
        INNER = HEADS * DIM_HEAD

        def rotate_half(x):
            x1 = x[..., ::2]
            x2 = x[..., 1::2]
            return jnp.concatenate((-x2, x1), axis=-1)

        def rope_fourier_cache(seq_len, head_dim, num_freqs):
            freqs = 10000.0 ** (-jnp.arange(0, head_dim, 2, dtype=jnp.float32) / head_dim)
            pos = jnp.arange(seq_len, dtype=jnp.float32)[:, None]
            angles = pos * freqs
            sin = jnp.sin(angles)
            cos = jnp.cos(angles)
            sin = jnp.stack([sin, sin], axis=-1).reshape(seq_len, head_dim)
            cos = jnp.stack([cos, cos], axis=-1).reshape(seq_len, head_dim)
            ffreqs = jnp.arange(1, num_freqs + 1, dtype=jnp.float32)
            p = jnp.arange(seq_len, dtype=jnp.float32)[:, None]
            fourier = jnp.concatenate([jnp.sin(p * ffreqs), jnp.cos(p * ffreqs)], axis=-1)
            return (sin, cos, fourier)
        key = jax.random.key(seed)
        ks = jax.random.split(key, 6)
        b, n = (4, 256)
        x = jax.random.normal(ks[0], (b, n, DIM), dtype=jnp.float32)
        w_qkv = jax.random.normal(ks[1], (3 * INNER, DIM), dtype=jnp.float32) * DIM ** (-0.5)
        w_fproj = jax.random.normal(ks[2], (DIM_HEAD, 2 * NUM_FREQS), dtype=jnp.float32) * (2 * NUM_FREQS) ** (-0.5)
        b_fproj = jax.random.normal(ks[3], (DIM_HEAD,), dtype=jnp.float32) * 0.02
        w_out = jax.random.normal(ks[4], (DIM, INNER), dtype=jnp.float32) * INNER ** (-0.5)
        b_out = jax.random.normal(ks[5], (DIM,), dtype=jnp.float32) * 0.02
        return {'x': x, 'w_qkv': w_qkv, 'w_fproj': w_fproj, 'b_fproj': b_fproj, 'w_out': w_out, 'b_out': b_out}
    _L0_attn_in = _L0_attn_setup()

    def _L0_ffn_setup():
        import jax, jax.numpy as jnp
        import numpy as np
        B, S, D = (4, 64, 128)
        E, K, H = (64, 8, 32)
        ES, HS = (2, 256)
        key = jax.random.key(seed)
        ks = jax.random.split(key, 8)
        scale = 0.02
        rn = lambda k, shape, s: jax.random.normal(k, shape, jnp.float32) * s
        return {'x': rn(ks[0], (B, S, D), 1.0), 'router_w': rn(ks[1], (D, E), scale), 'router_b': jnp.zeros((E,), jnp.float32), 'w1': rn(ks[2], (E, D, H), scale), 'b1': jnp.zeros((E, H), jnp.float32), 'w2': rn(ks[3], (E, H, D), scale), 'b2': jnp.zeros((E, D), jnp.float32), 'sw1': rn(ks[4], (ES, D, HS), scale), 'sb1': jnp.zeros((ES, HS), jnp.float32), 'sw2': rn(ks[5], (ES, HS, D), scale), 'sb2': jnp.zeros((ES, D), jnp.float32)}
    _L0_ffn_in = _L0_ffn_setup()
    _d = {'L0_attn_x': _L0_attn_in['x'], 'L0_attn_w_qkv': _L0_attn_in['w_qkv'], 'L0_attn_w_fproj': _L0_attn_in['w_fproj'], 'L0_attn_b_fproj': _L0_attn_in['b_fproj'], 'L0_attn_w_out': _L0_attn_in['w_out'], 'L0_attn_b_out': _L0_attn_in['b_out'], 'L0_ffn_router_w': _L0_ffn_in['router_w'], 'L0_ffn_router_b': _L0_ffn_in['router_b'], 'L0_ffn_w1': _L0_ffn_in['w1'], 'L0_ffn_b1': _L0_ffn_in['b1'], 'L0_ffn_w2': _L0_ffn_in['w2'], 'L0_ffn_b2': _L0_ffn_in['b2'], 'L0_ffn_sw1': _L0_ffn_in['sw1'], 'L0_ffn_sb1': _L0_ffn_in['sb1'], 'L0_ffn_sw2': _L0_ffn_in['sw2'], 'L0_ffn_sb2': _L0_ffn_in['sb2']}
    _x0 = _d['L0_attn_x']
    _d['L0_attn_x'] = jax.random.normal(jax.random.fold_in(jax.random.key(seed), 1), (1, 2048, 128), dtype=_x0.dtype)
    del _x0
    return _d

def reference(L0_attn_x, L0_attn_w_qkv, L0_attn_w_fproj, L0_attn_b_fproj, L0_attn_w_out, L0_attn_b_out, L0_ffn_router_w, L0_ffn_router_b, L0_ffn_w1, L0_ffn_b1, L0_ffn_w2, L0_ffn_b2, L0_ffn_sw1, L0_ffn_sb1, L0_ffn_sw2, L0_ffn_sb2):

    def _L0_attn_ref(x, w_qkv, w_fproj, b_fproj, w_out, b_out):
        import jax, jax.numpy as jnp
        import numpy as np
        DIM = 128
        HEADS = 16
        DIM_HEAD = 64
        NUM_FREQS = 16
        INNER = HEADS * DIM_HEAD

        def rotate_half(x):
            x1 = x[..., ::2]
            x2 = x[..., 1::2]
            return jnp.concatenate((-x2, x1), axis=-1)

        def rope_fourier_cache(seq_len, head_dim, num_freqs):
            freqs = 10000.0 ** (-jnp.arange(0, head_dim, 2, dtype=jnp.float32) / head_dim)
            pos = jnp.arange(seq_len, dtype=jnp.float32)[:, None]
            angles = pos * freqs
            sin = jnp.sin(angles)
            cos = jnp.cos(angles)
            sin = jnp.stack([sin, sin], axis=-1).reshape(seq_len, head_dim)
            cos = jnp.stack([cos, cos], axis=-1).reshape(seq_len, head_dim)
            ffreqs = jnp.arange(1, num_freqs + 1, dtype=jnp.float32)
            p = jnp.arange(seq_len, dtype=jnp.float32)[:, None]
            fourier = jnp.concatenate([jnp.sin(p * ffreqs), jnp.cos(p * ffreqs)], axis=-1)
            return (sin, cos, fourier)
        b, n, _ = x.shape
        scale = DIM_HEAD ** (-0.5)
        qkv = x @ w_qkv.T
        q, k, v = jnp.split(qkv, 3, axis=-1)

        def to_heads(t):
            return t.reshape(b, n, HEADS, DIM_HEAD).transpose(0, 2, 1, 3)
        q, k, v = (to_heads(q), to_heads(k), to_heads(v))
        sin, cos, fourier = rope_fourier_cache(n, DIM_HEAD, NUM_FREQS)
        fenc = fourier @ w_fproj.T + b_fproj
        fenc = fenc[None, None]
        q = q * cos + rotate_half(q) * sin + fenc
        k = k * cos + rotate_half(k) * sin + fenc
        dots = jnp.einsum('bhid,bhjd->bhij', q, k) * scale
        attn = jax.nn.softmax(dots, axis=-1)
        out = jnp.einsum('bhij,bhjd->bhid', attn, v)
        out = out.transpose(0, 2, 1, 3).reshape(b, n, INNER)
        return out @ w_out.T + b_out

    def _L0_ffn_ref(x, router_w, router_b, w1, b1, w2, b2, sw1, sb1, sw2, sb2):
        import jax, jax.numpy as jnp
        import numpy as np
        B, S, D = (4, 64, 128)
        E, K, H = (64, 8, 32)
        ES, HS = (2, 256)
        b_, s_, d_ = x.shape
        xf = x.reshape(-1, d_)
        probs = jax.nn.softmax(xf @ router_w + router_b, axis=-1)
        tw, ti = jax.lax.top_k(probs, K)
        tw = tw / jnp.sum(tw, axis=-1, keepdims=True)

        def body(acc, p):
            W1, B1, W2, B2, e = p
            h = jax.nn.silu(xf @ W1 + B1) @ W2 + B2
            cw = jnp.sum(jnp.where(ti == e, tw, 0.0), axis=-1)
            return (acc + cw[:, None] * h, None)
        routed, _ = jax.lax.scan(body, jnp.zeros_like(xf), (w1, b1, w2, b2, jnp.arange(w1.shape[0])))

        def shared_mlp(W1, B1, W2, B2):
            return jax.nn.silu(xf @ W1 + B1) @ W2 + B2
        shared = jnp.sum(jax.vmap(shared_mlp)(sw1, sb1, sw2, sb2), axis=0)
        return (routed + shared).reshape(b_, s_, d_)
    x = L0_attn_x
    xn = _layernorm(x, axis=-1)
    s = _L0_attn_ref(xn, L0_attn_w_qkv, L0_attn_w_fproj, L0_attn_b_fproj, L0_attn_w_out, L0_attn_b_out)
    g = _silu(_L0_ffn_ref(xn, L0_ffn_router_w, L0_ffn_router_b, L0_ffn_w1, L0_ffn_b1, L0_ffn_w2, L0_ffn_b2, L0_ffn_sw1, L0_ffn_sb1, L0_ffn_sw2, L0_ffn_sb2))
    x = x + s * g
    return x

_drawn_inputs = setup_inputs


def setup_inputs(seed=0):
    import zlib

    import numpy as np

    out = dict(_drawn_inputs(seed))
    spreads = {'L0_ffn_router_b': (0.0, 0.8),
     'L0_ffn_b1': (0.0, 0.8),
     'L0_ffn_b2': (0.0, 0.8),
     'L0_ffn_sb1': (0.0, 0.8),
     'L0_ffn_sb2': (0.0, 0.464)}
    factors = {'L0_attn_w_qkv': 3.442,
     'L0_attn_w_fproj': 4.466,
     'L0_attn_b_fproj': 8.0,
     'L0_attn_w_out': 2.935,
     'L0_attn_b_out': 22.693,
     'L0_ffn_router_w': 8.0,
     'L0_ffn_w1': 8.0,
     'L0_ffn_w2': 8.0,
     'L0_ffn_sw1': 8.0,
     'L0_ffn_sw2': 8.0}
    for name, (base, spread) in spreads.items():
        noise = np.random.default_rng([zlib.crc32(name.encode()), seed]).standard_normal(out[name].shape)
        drawn = base * np.exp(spread * noise) if base else spread * noise
        out[name] = jnp.asarray(drawn.astype(out[name].dtype))
    for name, factor in factors.items():
        out[name] = (out[name] * factor).astype(out[name].dtype)
    return out
```

```python
from contextlib import ExitStack

import numpy as np

import concourse.bass as bass
from concourse import mybir

F32 = mybir.dt.float32
F32R = mybir.dt.float32r
F16 = mybir.dt.float16
U32 = mybir.dt.uint32
ALU = mybir.AluOpType
ACT = mybir.ActivationFunctionType
AX = mybir.AxisListType
RMAX = bass.bass_isa.ReduceOp.absmax

P = 128
N = 2048
D = 128
NT = N // P
H = 16
DH = 64
PAIRS = H // 2
QC = 512
NQ = N // QC
QT = QC // P
STEPS = N // (2 * P)
UNITS = 2 * NQ
PAIR_STEPS = UNITS * STEPS
KC = N // 512
LEAD = 2
WCOLS = 5 * DH
E = 64
TOPK = 8
HID = 2560
NB = HID // P
NBR = 2048 // P
EPS = 1e-5
SCALE = DH ** -0.5
VW = 2 * DH + 2
OW = 2 * DH + 1
DMA = 16
MOVES = 12


def items(U, s, last):
    out = []
    qc, a = U % NQ, (U // NQ) % 2
    sl = STEPS * qc + s
    if not (last and U + 2 >= UNITS):
        out += [("max", U + 2, i // KC, i % KC) for i in (2 * s, 2 * s + 1)]
    if s == 1 and not (last and U + 1 >= UNITS):
        out.append(("turn_max", U + 1))
    if not (last and a == 1):
        if 1 <= sl <= 8:
            out.append(("proj" if sl % 2 else "rot", (sl - 1) // 2))
        if sl in (10, 12):
            out.append(("v", (sl - 10) // 2))
    if U > NQ and s == 4:
        out.append(("turn_o", (U - 1) % NQ))
    if U > NQ and s == 5:
        out.append(("out_proj", (U - 1) % NQ))
    return out


def head_items():
    return [(k, c) for c in range(4) for k in ("proj", "rot")] + [("v", 0), ("v", 1)]


def max_items(U):
    return [("max", U, i // KC, i % KC) for i in range(QT * KC)]


PRE = head_items() + max_items(0) + [("turn_max", 0)] + max_items(1)
A1 = len(PRE) + sum(len(items(0, s, False)) for s in range(STEPS))
AP = sum(len(items(U, s, False)) for U in range(1, UNITS + 1) for s in range(STEPS))


def program(nc, x, w_head, wv_all, wf, bf, four, cos, sin, w_out, b_out, rw, rb, w1, b1, w2, b2, sb2,
            expand, eye, out):
    ctx = ExitStack()
    with ctx:
        def sb(name, shape, dt, where=ctx):
            return where.enter_context(nc.sbuf_tensor(name, shape, dt))

        def sem(name):
            return ctx.enter_context(nc.semaphore(name))

        x_sb = sb("x_sb", [P, NT, D], F32)
        gate = sb("gate", [P, NT, D], F32)
        x_hi = sb("x_hi", [P, N], F32R)
        x_lo = sb("x_lo", [P, N], F32R)
        cos_sb = sb("cos_sb", [P, N], F32)
        sin_sb = sb("sin_sb", [P, N], F32)
        fenc = sb("fenc", [P, N], F32)
        eye_sb = sb("eye_sb", [P, P], F32)
        bout_sb = sb("bout_sb", [P, D], F32)
        vmax = sb("vmax", [P, 4], F32)
        early = ExitStack()
        xn = sb("xn", [P, NT, D], F32, early)
        stats = sb("stats", [P, NT, 6], F32, early)
        mv = sb("mv", [P, NT, 2], F32, early)
        rs = sb("rs", [P, 4, NT], F32, early)
        wv_sb = sb("wv_sb", [P, 1024], F32, early)
        four_sb = sb("four_sb", [32, N], F32, early)
        wf_sb = sb("wf_sb", [32, P], F32, early)
        bf_sb = sb("bf_sb", [P, 1], F32, early)
        rw_sb = sb("rw_sb", [P, E], F32, early)
        rw_hi = sb("rw_hi", [P, E], F32R, early)
        rw_lo = sb("rw_lo", [P, E], F32R, early)
        rb_sb = sb("rb_sb", [P, E], F32, early)
        logit = sb("logit", [P, NT, E], F32, early)
        prob = sb("prob", [P, NT, E], F32, early)
        rest = sb("rest", [P, NT, E], F32, early)
        top = sb("top", [P, NT, TOPK], F32, early)
        rstat = sb("rstat", [P, 5, NT], F32, early)
        cwt = sb("cwt", [P, NT, 2, E], F32, early)
        cw = sb("cw", [P, N], F32R, early)
        ex_in = sb("ex_in", [P, NBR, P], F32, early)
        ex = sb("ex", [P, NBR, P], F32R, early)
        w1_sb = sb("w1_sb", [P, HID], F32, early)
        w1_hi = sb("w1_hi", [P, HID], F32R, early)
        w1_lo = sb("w1_lo", [P, HID], F32R, early)
        b1_sb = sb("b1_sb", [P, NB], F32, early)
        w2_sb = sb("w2_sb", [P, NB, D], F32, early)
        b2_sb = sb("b2_sb", [P, D], F32, early)
        b2_hi = sb("b2_hi", [P, D], F32R, early)
        b2_lo = sb("b2_lo", [P, D], F32R, early)
        sb2_sb = sb("sb2_sb", [P, 2], F32, early)
        sb2_sum = sb("sb2_sum", [P, 1], F32, early)
        act_h = sb("act_h", [P, 2, 512], F32, early)
        hid = sb("hid", [P, 2, 512], F32, early)
        gate_t = sb("gate_t", [P, 512], F32, early)
        early.close()
        qm1 = [sb(f"qm1_{a}", [P, N], F32R) for a in range(2)]
        km1 = [sb(f"km1_{a}", [P, N], F32R) for a in range(2)]
        qm2 = [sb(f"qm2_{a}", [P, N], F32R) for a in range(2)]
        km2 = [sb(f"km2_{a}", [P, N], F32R) for a in range(2)]
        turn1 = sb("turn1", [P, 2, 512], F32)
        turn2 = sb("turn2", [P, 2, 512], F32)
        qk_hi = sb("qk_hi", [P, N], F32R)
        qk_lo = sb("qk_lo", [P, N], F32R)
        v_sb = [sb(f"v_{a}", [P, NT, VW], F16) for a in range(2)]
        w_in = sb("w_in", [P, WCOLS], F32)
        w_hi = sb("w_hi", [P, WCOLS], F32R)
        w_lo = sb("w_lo", [P, WCOLS], F32R)
        wo_sb = sb("wo_sb", [P, D], F32)
        pf = sb("pf", [P, 2, 2 * QC], F32)
        ph = sb("ph", [P, 4, 2 * QC], F16)
        pl = sb("pl", [P, 4, 2 * QC], F16)
        max_p = sb("max_p", [P, 2, QT, KC], F32)
        max_n = sb("max_n", [P, 2, QT], F32)
        max_r = sb("max_r", [QT, 2, 2, P], F32R)
        o_raw = sb("o_raw", [P, 2, QT, OW], F32)
        o_sum = sb("o_sum", [P, QT, DH], F32)
        o_rec = sb("o_rec", [P, 2, QT], F32)
        o_sb = sb("o_sb", [P, NT, 2 * DH], F32)
        ot_sb = sb("ot_sb", [P, QC], F32)
        s_acc = sb("s_acc", [P, NT, D], F32)

        ps_s = ctx.enter_context(nc.psum_tensor("ps_s", [P, 2, 2, 512], F32))
        ps_a = ctx.enter_context(nc.psum_tensor("ps_a", [P, 2, 512], F32))
        ps_o = ctx.enter_context(nc.psum_tensor("ps_o", [P, 2, 512], F32))

        ld_x, ld_mlp, ld_pos = sem("ld_x"), sem("ld_mlp"), sem("ld_pos")
        dve_seq = sem("dve_seq")
        var_ready, std_ready = sem("var_ready"), sem("std_ready")
        xn_ready, xt_ready, x_split = sem("xn_ready"), sem("xt_ready"), sem("x_split")
        fenc_ready = sem("fenc_ready")
        wvmax_ready, wvall_ready = sem("wvmax_ready"), sem("wvall_ready")
        logit_ready, shifted, exps = sem("logit_ready"), sem("shifted"), sem("exps")
        cw_tok, cw_turned, cw_ready = sem("cw_tok"), sem("cw_turned"), sem("cw_ready")
        h_ready, c_ready, sil_ready = sem("h_ready"), sem("c_ready"), sem("sil_ready")
        hid_ready, y_done = sem("hid_ready"), sem("y_done")
        gate_sil, gate_turned, gate_done = sem("gate_sil"), sem("gate_turned"), sem("gate_done")
        w_loaded, w_high, w_split = sem("w_loaded"), sem("w_high"), sem("w_split")
        wo_loaded = sem("wo_loaded")
        aux_ready, aux_free = sem("aux_ready"), sem("aux_free")
        v_high = sem("v_high")
        rope_a, rope_sum, hi_done, lo_done = sem("rope_a"), sem("rope_sum"), sem("hi_done"), sem("lo_done")
        moved, max_ready, max_high, max_rows = sem("moved"), sem("max_ready"), sem("max_high"), sem("max_rows")
        s_ready, probs_ready = sem("s_ready"), sem("probs_ready")
        pl_dve, pl_pool = sem("pl_dve"), sem("pl_pool")
        pv_done, acc_copied = sem("pv_done"), sem("acc_copied")
        rec_ready, osum_ready, o_ready = sem("rec_ready"), sem("osum_ready"), sem("o_ready")
        const_ready, fin, stored = sem("const_ready"), sem("fin"), sem("stored")

        MLP_LOADS = 13
        out_v = out[0].rearrange("(t p) d -> p t d", p=P)
        block = ctx.enter_context(nc.Block())

        @block.sync
        def _(sp):
            sp.dma_start(x_sb[:], x[0].rearrange("(t p) d -> p t d", p=P)).then_inc(ld_x, DMA)
            sp.dma_start(eye_sb[:], eye).then_inc(ld_x, DMA)
            for dst, src in ((rw_sb, rw), (rb_sb, rb), (wf_sb, wf), (bf_sb, bf), (four_sb, four),
                             (wv_sb, wv_all), (w1_sb, w1), (b1_sb, b1), (ex_in, expand), (w2_sb, w2),
                             (b2_sb, b2), (sb2_sb, sb2), (bout_sb, b_out)):
                sp.dma_start(dst[:], src).then_inc(ld_mlp, DMA)
            sp.dma_start(cos_sb[:], cos).then_inc(ld_pos, DMA)
            sp.dma_start(sin_sb[:], sin).then_inc(ld_pos, DMA)
            sp.wait_ge(gate_done, 4)
            sp.dma_start(w_in[:], w_head[0]).then_inc(w_loaded, DMA)

            def move_half(half, a, chunks):
                sp.wait_ge(lo_done, chunks)
                c = slice(half * 1024, half * 1024 + 1024)
                for dst, src, p0 in ((qm1[a][0:DH, c], qk_hi, 0), (qm1[a][DH:P, c], qk_lo, 0),
                                     (km1[a][0:DH, c], qk_hi, DH), (km1[a][DH:P, c], qk_hi, DH),
                                     (qm2[a][0:DH, c], qk_hi, 0), (km2[a][0:DH, c], qk_lo, DH)):
                    sp.dma_start(dst.bitcast(F32), src[p0:p0 + DH, c].bitcast(F32)).then_inc(moved, DMA)

            def max_row(U, consumed):
                a, qc = (U // NQ) % 2, U % NQ
                sp.wait_ge(aux_free, consumed)
                for part in range(2):
                    sp.dma_start(qm2[a][DH + part:DH + part + 1, qc * QC:(qc + 1) * QC].bitcast(F32)
                                 .rearrange("o (t q) -> o t q", t=QT),
                                 max_r[:, U % 2, part, :].bitcast(F32)).then_inc(max_rows, DMA)

            def unit(U, g, k, last):
                qc, hd = U % NQ, U // NQ
                a = hd % 2
                if U == 1:
                    sp.wait_ge(aux_ready, k + AP * g)
                    sp.dma_start(wo_sb[:], w_out[g]).then_inc(wo_loaded, DMA)
                for s in range(STEPS):
                    for it in items(U, s, last):
                        k += 1
                        if it[0] == "turn_max":
                            max_row(it[1], k + AP * g)
                if qc == 0 and not (last and a == 1):
                    move_half(0, 1 - a, 4 * (hd + 1) + 2 + 8 * g)
                if qc == 1:
                    if not (last and a == 1):
                        move_half(1, 1 - a, 4 * (hd + 1) + 4 + 8 * g)
                    if not last:
                        sp.wait_ge(w_split, hd + 2 + 2 * g)
                        sp.dma_start(w_in[:], w_head[g * 2 + (hd + 2)]).then_inc(w_loaded, DMA)
                return k

            move_half(0, 0, 2)
            move_half(1, 0, 4)
            sp.wait_ge(w_split, 1)
            sp.dma_start(w_in[:], w_head[1]).then_inc(w_loaded, DMA)
            k = 0
            for it in PRE:
                k += 1
                if it[0] == "turn_max":
                    max_row(0, k)
            k = unit(0, 0, k, False)
            with sp.Fori(0, PAIRS - 1) as g:
                kk = k
                for U in range(1, UNITS + 1):
                    kk = unit(U, g, kk, False)
            for U in range(1, UNITS):
                k = unit(U, PAIRS - 1, k, True)
            for c in range(NQ):
                sp.wait_ge(fin, c + 1)
                sp.dma_start(out_v[:, QT * c:QT * c + QT, :], o_sb[:, QT * c:QT * c + QT, :]).then_inc(stored, DMA)
            sp.wait_ge(stored, NQ * DMA)

        @block.tensor
        def _(pe):
            mm = nc.tensor.matmul

            def mm3(dst, s_hi, s_lo, m_hi, m_lo, start=True, stop=True):
                mm(dst, s_hi, m_hi, start=start, stop=False)
                mm(dst, s_lo, m_hi, start=False, stop=False)
                return mm(dst, s_hi, m_lo, start=False, stop=stop)

            pe.wait_ge(ld_x, 2 * DMA)
            for c in range(4):
                pe.wait_ge(xn_ready, c + 1)
                for i in range(4):
                    last = nc.tensor.transpose(ps_s[:, c // 2, c % 2, i * P:(i + 1) * P], xn[:, 4 * c + i, :], eye_sb[:])
                last.then_inc(xt_ready, 1)
            pe.wait_ge(x_split, 4)
            pe.wait_ge(ld_mlp, MLP_LOADS * DMA)
            for c in range(4):
                mm(ps_s[:, c // 2, c % 2, :], wf_sb[:], four_sb[:, c * 512:(c + 1) * 512], start=True, stop=True)\
                    .then_inc(fenc_ready, 1)
            pe.wait_ge(dve_seq, 1)
            for i in range(NT):
                dst = ps_o[:, i // 8, (i % 8) * E:(i % 8 + 1) * E]
                t = slice(i * P, (i + 1) * P)
                mm3(dst, x_hi[:, t], x_lo[:, t], rw_hi[:], rw_lo[:], stop=False)
                last = mm(dst, x_lo[:, t], rw_lo[:], start=False, stop=True)
            last.then_inc(logit_ready, 1)
            pe.wait_ge(cw_tok, 1)
            for c in range(4):
                if c >= 2:
                    pe.wait_ge(cw_ready, c - 1)
                for i in range(4):
                    last = nc.tensor.transpose(ps_a[:, c % 2, i * P:(i + 1) * P], cwt[:, 4 * c + i, :, :], eye_sb[:])
                last.then_inc(cw_turned, 1)
            pe.wait_ge(cw_ready, 4)

            with pe.Fori(0, 4) as tc:
                tok = bass.ts(tc, 512)

                def down(j):
                    if j < NBR:
                        pe.wait_ge(hid_ready, tc * NBR + (j + 1))
                    else:
                        pe.wait_ge(sil_ready, tc * NB + (j + 1))
                    mm(ps_o[:, 0, :], w2_sb[:, j, :], hid[:, j % 2, :], start=False, stop=(j == NB - 1))\
                        .then_inc(y_done, 1)

                mm(ps_o[:, 0, :], b2_hi[:], cw[:, tok], start=True, stop=False)
                mm(ps_o[:, 0, :], b2_lo[:], cw[:, tok], start=False, stop=False)
                for j in range(NB):
                    if j >= 2:
                        pe.wait_ge(sil_ready, tc * NB + (j - 1))
                    c = slice(j * P, (j + 1) * P)
                    mm3(ps_s[:, j % 2, 0, :], w1_hi[:, c], w1_lo[:, c], x_hi[:, tok], x_lo[:, tok]).then_inc(h_ready, 1)
                    if j < NBR:
                        mm(ps_s[:, j % 2, 1, :], ex[:, j, :], cw[:, tok], start=True, stop=True).then_inc(c_ready, 1)
                    if j >= 1:
                        down(j - 1)
                down(NB - 1)
                pe.wait_ge(gate_sil, tc + 1)
                for i in range(4):
                    last = nc.tensor.transpose(ps_a[:, 0, i * P:(i + 1) * P], gate_t[:, i * P:(i + 1) * P], eye_sb[:])
                last.then_inc(gate_turned, 1)

            pe.wait_ge(gate_done, 4)

            def aux(it, k, g, hn, wo_count):
                kind, bank = it[0], k % 2
                dst = ps_a[:, bank, :]
                if k >= 2:
                    pe.wait_ge(aux_free, k - 1 + AP * g)
                if kind == "max":
                    _, U, qt, kc = it
                    a, qc = (U // NQ) % 2, U % NQ
                    if qc == 0 and qt == 0 and kc == 0:
                        pe.wait_ge(moved, DMA * MOVES * (U // NQ + 1) + 2 * DMA * MOVES * g)
                    q0 = qc * QC + qt * P
                    last = mm(dst, qm1[a][:, q0:q0 + P], km1[a][:, kc * 512:(kc + 1) * 512], start=True, stop=True)
                elif kind == "turn_max":
                    U = it[1]
                    pe.wait_ge(max_ready, U + 1 + UNITS * g)
                    last = mm(ps_a[0:QT, bank, 0:P], max_n[:, U % 2, :], eye_sb[:], start=True, stop=True)
                elif kind in ("proj", "rot"):
                    if it == ("proj", 0):
                        pe.wait_ge(w_split, hn + 1)
                    w = slice(0, P) if kind == "proj" else slice(P, 2 * P)
                    t = slice(it[1] * 512, (it[1] + 1) * 512)
                    last = mm3(dst, w_hi[:, w], w_lo[:, w], x_hi[:, t], x_lo[:, t])
                elif kind == "v":
                    for i in range(8):
                        t = slice((8 * it[1] + i) * P, (8 * it[1] + i + 1) * P)
                        last = mm3(dst[:, i * DH:(i + 1) * DH], x_hi[:, t], x_lo[:, t], w_hi[:, 2 * P:], w_lo[:, 2 * P:])
                elif kind == "turn_o":
                    pe.wait_ge(o_ready, NQ + it[1] + 1 + UNITS * g)
                    for i in range(QT):
                        last = nc.tensor.transpose(dst[:, i * P:(i + 1) * P], o_sb[:, QT * it[1] + i, :], eye_sb[:])
                else:
                    pe.wait_ge(aux_free, k + AP * g)
                    pe.wait_ge(wo_loaded, wo_count)
                    for i in range(QT):
                        last = mm(dst[:, i * P:(i + 1) * P], ot_sb[:, i * P:(i + 1) * P], wo_sb[:], start=True, stop=True)
                last.then_inc(aux_ready, 1)

            def scores(L, g):
                U = L // STEPS
                a, qc = (U // NQ) % 2, U % NQ
                if L % STEPS == 0:
                    if qc == 0:
                        pe.wait_ge(moved, DMA * MOVES * (U // NQ + 1) + 2 * DMA * MOVES * g)
                    pe.wait_ge(max_rows, 2 * DMA * (U + 1) + 2 * DMA * UNITS * g)
                if L >= 2:
                    pe.wait_ge(probs_ready, L - 1 + PAIR_STEPS * g)
                q = slice(qc * QC, (qc + 1) * QC)
                for i in range(2):
                    kt = slice((2 * (L % STEPS) + i) * P, (2 * (L % STEPS) + i + 1) * P)
                    mm(ps_s[:, L % 2, i, :], km1[a][:, kt], qm1[a][:, q], start=True, stop=False)
                    last = mm(ps_s[:, L % 2, i, :], km2[a][0:DH + 2, kt], qm2[a][0:DH + 2, q], start=False, stop=True)
                last.then_inc(s_ready, 1)

            def times_v(L, g, first, count):
                U = L // STEPS
                a = (U // NQ) % 2
                if first == 0:
                    if L % STEPS == 0 and not (isinstance(g, int) and U + UNITS * g == 0):
                        pe.wait_ge(acc_copied, U + UNITS * g)
                    pe.wait_ge(pl_pool if L % 2 else pl_dve, L // 2 + 1 + PAIR_STEPS // 2 * g)
                for n in range(first, first + count):
                    i, qt = n // QT, n % QT
                    kt = 2 * (L % STEPS) + i
                    dst = ps_o[:, qt // 2, (qt % 2) * 256:(qt % 2) * 256 + OW]
                    c = slice(i * QC + qt * P, i * QC + (qt + 1) * P)
                    mm(dst, ph[:, L % 4, c], v_sb[a][:, kt, 0:OW], start=(kt == 0 and qt % 2 == 0),
                       stop=False, skip_group_check=True)
                    last = mm(dst, pl[:, L % 4, c], v_sb[a][:, kt, 0:OW], start=False,
                              stop=(kt == NT - 1), skip_group_check=True)
                if first + count == 2 * QT:
                    last.then_inc(pv_done, 1)

            def unit(U, g, k, last):
                for s in range(STEPS):
                    L = U * STEPS + s
                    if not (last and L + LEAD >= PAIR_STEPS):
                        scores(L + LEAD, g)
                    work = items(U, s, last)
                    done = 0
                    for n, it in enumerate(work):
                        aux(it, k, g, U // NQ + 1 + 2 * g, DMA * (g + 1))
                        k += 1
                        upto = (n + 1) * 2 * QT // len(work)
                        if upto > done:
                            times_v(L, g, done, upto - done)
                            done = upto
                    if done < 2 * QT:
                        times_v(L, g, done, 2 * QT - done)
                return k

            k = 0
            for it in PRE:
                aux(it, k, 0, 0, 0)
                k += 1
            pe.wait_ge(const_ready, 4)
            scores(0, 0)
            scores(1, 0)
            k = unit(0, 0, k, False)
            with pe.Fori(0, PAIRS - 1) as g:
                kk = k
                for U in range(1, UNITS + 1):
                    kk = unit(U, g, kk, False)
            for U in range(1, UNITS):
                k = unit(U, PAIRS - 1, k, True)
            for it in (("turn_o", NQ - 1), ("out_proj", NQ - 1)):
                aux(it, k, PAIRS - 1, 0, DMA * PAIRS)
                k += 1

        @block.scalar
        def _(act):
            act.wait_ge(var_ready, 1)
            nc.scalar.activation(rs[:, 1, :], rs[:, 0, :], ACT.Sqrt).then_inc(std_ready, 1)
            act.wait_ge(shifted, 1)
            nc.scalar.activation(prob[:], logit[:], ACT.Exp).then_inc(exps, 1)
            act.wait_ge(cw_ready, 4)
            with act.Fori(0, 4) as tc:
                for j in range(NB):
                    act.wait_ge(h_ready, tc * NB + (j + 1))
                    if j < NBR:
                        if j >= 2:
                            act.wait_ge(hid_ready, tc * NBR + (j - 1))
                        dst = act_h[:, j % 2, :]
                    else:
                        act.wait_ge(y_done, tc * NB + (j - 1))
                        dst = hid[:, j % 2, :]
                    nc.scalar.activation(dst, ps_s[:, j % 2, 0, :], ACT.Silu, bias=b1_sb[:, j:j + 1]).then_inc(sil_ready, 1)
                act.wait_ge(y_done, tc * NB + NB)
                nc.scalar.activation(gate_t[:], ps_o[:, 0, :], ACT.Silu, bias=sb2_sum[:, 0:1]).then_inc(gate_sil, 1)
            act.wait_ge(gate_done, 4)

            def exp_step(L, g):
                act.wait_ge(s_ready, L + 1 + PAIR_STEPS * g)
                if L >= 2:
                    act.wait_ge(pl_pool if L % 2 else pl_dve, L // 2 + PAIR_STEPS // 2 * g)
                if L >= 4:
                    act.wait_ge(pv_done, L - 3 + PAIR_STEPS * g)
                nc.scalar.activation(pf[:, L % 2, :].rearrange("p (i q) -> p i q", i=2), ps_s[:, L % 2, :, :],
                                     ACT.Exp, scale=SCALE)
                nc.scalar.activation(ph[:, L % 4, :].rearrange("p (i q) -> p i q", i=2), ps_s[:, L % 2, :, :],
                                     ACT.Exp, scale=SCALE).then_inc(probs_ready, 1)

            def take_sums(U, g):
                act.wait_ge(pv_done, STEPS * U + PAIR_STEPS * g)
                nc.scalar.activation(o_raw[:, (U - 1) % 2, :, :].rearrange("p (b i) c -> p b i c", b=2),
                                     ps_o[:].rearrange("p b (i c) -> p b i c", i=2)[:, :, :, 0:OW],
                                     ACT.Copy).then_inc(acc_copied, 1)

            def unit(U, g, last):
                for s in range(STEPS):
                    L = U * STEPS + s
                    if s == 0 and not (isinstance(g, int) and U + UNITS * g == 0):
                        take_sums(U, g)
                    if not (last and L + LEAD >= PAIR_STEPS):
                        exp_step(L + LEAD, g)

            exp_step(0, 0)
            exp_step(1, 0)
            unit(0, 0, False)
            with act.Fori(0, PAIRS - 1) as g:
                for U in range(1, UNITS + 1):
                    unit(U, g, False)
            for U in range(1, UNITS):
                unit(U, PAIRS - 1, True)
            take_sums(UNITS, PAIRS - 1)

        @block.vector
        def _(dve):
            V = nc.vector
            seq = [0]

            def link(ins):
                seq[0] += 1
                ins.then_inc(dve_seq, 1)
                dve.wait_ge(dve_seq, seq[0])

            dve.wait_ge(ld_mlp, MLP_LOADS * DMA)
            V.tensor_copy(rw_hi[:], rw_sb[:]).then_inc(w_high, 1)
            dve.wait_ge(w_high, 1)
            link(V.tensor_tensor(rw_lo[:], rw_sb[:], rw_hi[:].bitcast(F32), ALU.subtract))
            dve.wait_ge(ld_x, 2 * DMA)
            for i in range(NT):
                st = V.bn_stats(stats[:, i, :], x_sb[:, i, :])
            link(st)
            for i in range(NT):
                st = V.bn_aggr(mv[:, i, :], stats[:, i, :])
            link(st)
            V.tensor_scalar(rs[:, 0, :], mv[:, :, 1], EPS, None, ALU.add).then_inc(var_ready, 1)
            dve.wait_ge(std_ready, 1)
            link(V.reciprocal(rs[:, 2, :], rs[:, 1, :]))
            link(V.tensor_tensor(rs[:, 3, :], rs[:, 2, :], rs[:, 2, :], ALU.mult))
            link(V.tensor_tensor(rs[:, 1, :], rs[:, 3, :], rs[:, 0, :], ALU.mult))
            link(V.tensor_scalar(rs[:, 3, :], rs[:, 1, :], -0.5, 1.5, ALU.mult, ALU.add))
            link(V.tensor_tensor(rs[:, 1, :], rs[:, 3, :], rs[:, 2, :], ALU.mult))
            for i in range(NT):
                ins = V.tensor_scalar(xn[:, i, :], x_sb[:, i, :], mv[:, i, 0:1], rs[:, 1, i:i + 1], ALU.subtract, ALU.mult)
                if i % 4 == 3:
                    ins.then_inc(xn_ready, 1)
            for c in range(4):
                dve.wait_ge(xt_ready, c + 1)
                t = slice(c * 512, (c + 1) * 512)
                link(V.tensor_copy(x_hi[:, t], ps_s[:, c // 2, c % 2, :]))
                V.tensor_tensor(x_lo[:, t], ps_s[:, c // 2, c % 2, :], x_hi[:, t].bitcast(F32), ALU.subtract)\
                    .then_inc(x_split, 1)
            link(V.tensor_copy(w1_hi[:], w1_sb[:]))
            V.tensor_tensor(w1_lo[:], w1_sb[:], w1_hi[:].bitcast(F32), ALU.subtract)
            V.tensor_copy(ex[:], ex_in[:])
            link(V.tensor_copy(b2_hi[:], b2_sb[:]))
            V.tensor_tensor(b2_lo[:], b2_sb[:], b2_hi[:].bitcast(F32), ALU.subtract)
            V.tensor_tensor(sb2_sum[:], sb2_sb[:, 0:1], sb2_sb[:, 1:2], ALU.add)
            for c in range(4):
                dve.wait_ge(fenc_ready, c + 1)
                V.tensor_scalar(fenc[:, c * 512:(c + 1) * 512], ps_s[:, c // 2, c % 2, :], bf_sb[:, 0:1], None, ALU.add)
            V.tensor_reduce(vmax[:, 0:1], wv_sb[:], AX.X, ALU.max, apply_absolute_value=True).then_inc(wvmax_ready, 1)
            dve.wait_ge(logit_ready, 1)
            for b in range(2):
                ins = V.tensor_tensor(logit[:, 8 * b:8 * b + 8, :], ps_o[:, b, :].rearrange("p (t e) -> p t e", t=8),
                                      rb_sb[:].unsqueeze(1).to_broadcast([P, 8, E]), ALU.add)
            link(ins)
            link(V.tensor_reduce(rstat[:, 0, :], logit[:], AX.X, ALU.max))
            V.tensor_tensor(logit[:], logit[:], rstat[:, 0, :].unsqueeze(2).to_broadcast([P, NT, E]), ALU.subtract)\
                .then_inc(shifted, 1)
            dve.wait_ge(exps, 1)
            link(V.tensor_reduce(rstat[:, 1, :], prob[:], AX.X, ALU.add))
            link(V.reciprocal(rstat[:, 2, :], rstat[:, 1, :]))
            link(V.tensor_tensor(prob[:], prob[:], rstat[:, 2, :].unsqueeze(2).to_broadcast([P, NT, E]), ALU.mult))
            for i in range(NT):
                ins = V.max(top[:, i, :], prob[:, i, :])
            link(ins)
            for i in range(NT):
                ins = V.match_replace(rest[:, i, :], top[:, i, :], prob[:, i, :], 0.0)
            link(ins)
            V.tensor_tensor(logit[:], prob[:], rest[:], ALU.subtract)
            link(V.tensor_reduce(rstat[:, 3, :], top[:], AX.X, ALU.add))
            link(V.reciprocal(rstat[:, 4, :], rstat[:, 3, :]))
            for i in range(2):
                ins = V.tensor_tensor(cwt[:, :, i, :], logit[:], rstat[:, 4, :].unsqueeze(2).to_broadcast([P, NT, E]), ALU.mult)
            ins.then_inc(cw_tok, 1)
            for c in range(4):
                dve.wait_ge(cw_turned, c + 1)
                t = slice(c * 512, (c + 1) * 512)
                link(V.tensor_copy(cw[:, t], ps_a[:, c % 2, :]))
                V.tensor_tensor(cw[E:, t], ps_a[E:, c % 2, :], cw[E:, t].bitcast(F32), ALU.subtract).then_inc(cw_ready, 1)

            with dve.Fori(0, 4) as tc:
                for j in range(NBR):
                    dve.wait_ge(sil_ready, tc * NB + (j + 1))
                    dve.wait_ge(c_ready, tc * NBR + (j + 1))
                    if j >= 2:
                        dve.wait_ge(y_done, tc * NB + (j - 1))
                    V.tensor_tensor(hid[:, j % 2, :], ps_s[:, j % 2, 1, :], act_h[:, j % 2, :], ALU.mult)\
                        .then_inc(hid_ready, 1)
                dve.wait_ge(gate_turned, tc + 1)
                V.tensor_copy(gate[:, bass.ts(tc, 4), :], ps_a[:, 0, :].rearrange("p (t d) -> p t d", t=4))\
                    .then_inc(gate_done, 1)

            dve.wait_ge(gate_done, 4)
            dve.wait_ge(ld_pos, 2 * DMA)
            dve.wait_ge(wvall_ready, 1)
            link(V.tensor_scalar(vmax[:, 2:3], vmax[:, 1:2], 2.0 ** -100, None, ALU.max))
            link(V.tensor_single_scalar(vmax[:, 2:3].bitcast(U32), vmax[:, 2:3].bitcast(U32), 0x7F800000, ALU.bitwise_and))
            link(V.reciprocal(vmax[:, 3:4], vmax[:, 2:3]))
            link(V.memset(s_acc[:], 0.0))

            def split_weights(hn):
                dve.wait_ge(w_loaded, DMA * (hn + 1))
                V.tensor_copy(w_hi[:], w_in[:]).then_inc(w_high, 1)
                dve.wait_ge(w_high, hn + 2)
                V.tensor_tensor(w_lo[:], w_in[:], w_hi[:].bitcast(F32), ALU.subtract).then_inc(w_split, 1)

            def combine_max(U, g, k):
                dve.wait_ge(aux_free, k)
                V.tensor_reduce(max_n[:, U % 2, :], max_p[:, U % 2, :, :], AX.X, ALU.max, negate=True).then_inc(max_ready, 1)

            def high_part(c, hn, first):
                if c == 0 and not first:
                    dve.wait_ge(moved, DMA * MOVES * hn)
                dve.wait_ge(rope_sum, 4 * hn + c + 1)
                V.tensor_copy(qk_hi[:, c * 512:(c + 1) * 512], turn1[:, c % 2, :]).then_inc(hi_done, 1)

            def low_probs(L, g):
                dve.wait_ge(probs_ready, L + 1 + PAIR_STEPS * g)
                V.tensor_tensor(pl[:, L % 4, :], pf[:, L % 2, :], ph[:, L % 4, :], ALU.subtract).then_inc(pl_dve, 1)

            def aux(it, k, g, hn, first, vpar):
                kind = it[0]
                src = ps_a[:, k % 2, :]
                dve.wait_ge(aux_ready, k + 1 + AP * g)
                if kind == "max":
                    _, U, qt, kc = it
                    V.tensor_reduce(max_p[:, U % 2, qt, kc:kc + 1], src, AX.X, ALU.max).then_inc(aux_free, 1)
                elif kind == "turn_max":
                    U = it[1]
                    if not (isinstance(g, int) and U + UNITS * g < 2):
                        dve.wait_ge(max_rows, 2 * DMA * (U - 1) + 2 * DMA * UNITS * g)
                    src = ps_a[0:QT, k % 2, 0:P]
                    V.tensor_copy(max_r[:, U % 2, 0, :], src).then_inc(max_high, 1)
                    dve.wait_ge(max_high, U + 1 + UNITS * g)
                    V.tensor_tensor(max_r[:, U % 2, 1, :], src, max_r[:, U % 2, 0, :].bitcast(F32), ALU.subtract)\
                        .then_inc(aux_free, 1)
                elif kind == "proj":
                    c = it[1]
                    if not (first and c < 2):
                        dve.wait_ge(lo_done, 4 * hn + (c - 1))
                    V.tensor_tensor(turn1[:, c % 2, :], src, cos_sb[:, c * 512:(c + 1) * 512], ALU.mult).then_inc(aux_free, 1)
                elif kind == "rot":
                    c = it[1]
                    V.tensor_tensor(turn2[:, c % 2, :], src, sin_sb[:, c * 512:(c + 1) * 512], ALU.mult).then_inc(aux_free, 1)
                elif kind == "v":
                    src = src.rearrange("p (t d) -> p t d", t=8)
                    t = slice(8 * it[1], 8 * it[1] + 8)
                    V.tensor_scalar(v_sb[vpar][:, t, 0:DH], src, vmax[:, 3:4], None, ALU.mult).then_inc(v_high, 1)
                    dve.wait_ge(v_high, 2 * hn + (it[1] + 1))
                    V.scalar_tensor_tensor(out=v_sb[vpar][:, t, DH:2 * DH], in0=src, scalar=vmax[:, 3:4],
                                           in1=v_sb[vpar][:, t, 0:DH], op0=ALU.mult, op1=ALU.subtract).then_inc(aux_free, 1)
                elif kind == "turn_o":
                    V.tensor_copy(ot_sb[:], src).then_inc(aux_free, 1)
                else:
                    t = slice(QT * it[1], QT * it[1] + QT)
                    V.tensor_tensor(s_acc[:, t, :], src.rearrange("p (t d) -> p t d", t=QT), s_acc[:, t, :], ALU.add)\
                        .then_inc(aux_free, 1)

            def take_rec(U, g):
                dve.wait_ge(acc_copied, U + UNITS * g)
                V.reciprocal(o_rec[:, (U - 1) % 2, :], o_raw[:, (U - 1) % 2, :, 2 * DH]).then_inc(rec_ready, 1)

            def unit(U, g, k, last):
                hd = U // NQ
                hn = hd + 1 + 2 * g
                prep = not (last and hd % 2 == 1)
                for s in range(STEPS):
                    L = U * STEPS + s
                    sl = STEPS * (U % NQ) + s
                    if s == 0 and not (last and U + 1 >= UNITS):
                        combine_max(U + 1, g, k + AP * g)
                    if sl == 0 and prep:
                        split_weights(hn)
                    for it in items(U, s, last):
                        aux(it, k, g, hn, False, 1 - hd % 2)
                        k += 1
                    if sl in (3, 5, 7, 9) and prep:
                        high_part((sl - 3) // 2, hn, False)
                    if s == 1 and not (isinstance(g, int) and U + UNITS * g == 0):
                        take_rec(U, g)
                    if (L + 1) % 2 == 0 and not (last and L + 1 >= PAIR_STEPS):
                        low_probs(L + 1, g)
                return k

            split_weights(0)
            k = 0
            for it in PRE:
                aux(it, k, 0, 0, True, 0)
                k += 1
                if it[0] == "rot":
                    high_part(it[1], 0, True)
                if it == ("max", 0, QT - 1, KC - 1):
                    combine_max(0, 0, k)
            low_probs(0, 0)
            k = unit(0, 0, k, False)
            with dve.Fori(0, PAIRS - 1) as g:
                kk = k
                for U in range(1, UNITS + 1):
                    kk = unit(U, g, kk, False)
            for U in range(1, UNITS):
                k = unit(U, PAIRS - 1, k, True)
            take_rec(UNITS, PAIRS - 1)
            for it in (("turn_o", NQ - 1), ("out_proj", NQ - 1)):
                aux(it, k, PAIRS - 1, 0, False, 0)
                k += 1
            dve.wait_ge(aux_free, k + AP * (PAIRS - 1))
            for c in range(NQ):
                t = slice(QT * c, QT * c + QT)
                link(V.scalar_tensor_tensor(out=s_acc[:, t, :], in0=s_acc[:, t, :], scalar=vmax[:, 2:3],
                                            in1=bout_sb[:].unsqueeze(1).to_broadcast([P, QT, D]),
                                            op0=ALU.mult, op1=ALU.add))
                link(V.tensor_tensor(s_acc[:, t, :], s_acc[:, t, :], gate[:, t, :], ALU.mult))
                V.tensor_tensor(o_sb[:, t, :], s_acc[:, t, :], x_sb[:, t, :], ALU.add).then_inc(fin, 1)

        @block.gpsimd
        def _(pool):
            G = nc.gpsimd
            pool.wait_ge(wvmax_ready, 1)
            G.partition_all_reduce(vmax[:, 1:2], vmax[:, 0:1], P, RMAX).then_inc(wvall_ready, 1)
            pool.wait_ge(wvall_ready, 1)
            pool.wait_ge(gate_done, 4)
            for a in range(2):
                G.memset(km2[a][DH:DH + 2, :].bitcast(F32), 1.0).then_inc(const_ready, 1)
                pool.wait_ge(const_ready, 2 * a + 1)
                G.memset(v_sb[a][:, :, 2 * DH:VW], 1.0).then_inc(const_ready, 1)
                pool.wait_ge(const_ready, 2 * a + 2)

            def rope_add(c, hn, k):
                pool.wait_ge(aux_free, k)
                G.tensor_tensor(turn2[:, c % 2, :], turn2[:, c % 2, :], fenc[:, c * 512:(c + 1) * 512], ALU.add).then_inc(rope_a, 1)
                pool.wait_ge(rope_a, 4 * hn + c + 1)
                G.tensor_tensor(turn1[:, c % 2, :], turn1[:, c % 2, :], turn2[:, c % 2, :], ALU.add).then_inc(rope_sum, 1)

            def low_part(c, hn):
                pool.wait_ge(hi_done, 4 * hn + c + 1)
                G.tensor_tensor(qk_lo[:, c * 512:(c + 1) * 512], turn1[:, c % 2, :],
                                qk_hi[:, c * 512:(c + 1) * 512].bitcast(F32), ALU.subtract).then_inc(lo_done, 1)

            def low_probs(L, g):
                pool.wait_ge(probs_ready, L + 1 + PAIR_STEPS * g)
                G.tensor_tensor(pl[:, L % 4, :], pf[:, L % 2, :], ph[:, L % 4, :], ALU.subtract).then_inc(pl_pool, 1)

            def add_parts(U, g):
                pool.wait_ge(acc_copied, U + UNITS * g)
                r = o_raw[:, (U - 1) % 2, :, :]
                G.tensor_tensor(o_sum[:], r[:, :, 0:DH], r[:, :, DH:2 * DH], ALU.add).then_inc(osum_ready, 1)

            def normalise(U, g):
                pool.wait_ge(rec_ready, U + UNITS * g)
                pool.wait_ge(osum_ready, U + UNITS * g)
                qc, a = (U - 1) % NQ, ((U - 1) // NQ) % 2
                G.tensor_tensor(o_sb[:, QT * qc:QT * qc + QT, a * DH:(a + 1) * DH], o_sum[:],
                                o_rec[:, (U - 1) % 2, :].unsqueeze(2).to_broadcast([P, QT, DH]), ALU.mult).then_inc(o_ready, 1)

            def unit(U, g, k, last):
                hd = U // NQ
                hn = hd + 1 + 2 * g
                prep = not (last and hd % 2 == 1)
                rot_k = 0
                for s in range(STEPS):
                    L = U * STEPS + s
                    sl = STEPS * (U % NQ) + s
                    post = not (isinstance(g, int) and U + UNITS * g == 0)
                    if (L + 1) % 2 == 1 and not (last and L + 1 >= PAIR_STEPS):
                        low_probs(L + 1, g)
                    for it in items(U, s, last):
                        k += 1
                        if it[0] == "rot":
                            rot_k = k
                    if prep and sl in (3, 5, 7):
                        rope_add((sl - 3) // 2, hn, rot_k + AP * g)
                    if prep and sl == 9:
                        rope_add(3, hn, rot_k + AP * g)
                    if prep and sl in (4, 6, 8, 10):
                        low_part((sl - 4) // 2, hn)
                    if s == 1 and post:
                        add_parts(U, g)
                    if s == 2 and post:
                        normalise(U, g)
                return k

            k = 0
            for it in PRE:
                k += 1
                if it[0] == "rot":
                    rope_add(it[1], 0, k)
                    low_part(it[1], 0)
            k = unit(0, 0, k, False)
            with pool.Fori(0, PAIRS - 1) as g:
                kk = k
                for U in range(1, UNITS + 1):
                    kk = unit(U, g, kk, False)
            for U in range(1, UNITS):
                k = unit(U, PAIRS - 1, k, True)
            add_parts(UNITS, PAIRS - 1)
            normalise(UNITS, PAIRS - 1)


def constants():
    freqs = (10000.0 ** (-np.arange(0, DH, 2, dtype=np.float64) / DH)).astype(np.float32)
    pos = np.arange(N, dtype=np.float32)[:, None]
    ang = (pos * freqs).astype(np.float64)
    cos = np.repeat(np.cos(ang), 2, axis=1).T.astype(np.float32)
    sin = np.repeat(np.sin(ang), 2, axis=1).T.astype(np.float32)
    sin[:DH // 2] *= -1
    ff = (pos * np.arange(1, 17, dtype=np.float32)).astype(np.float64)
    four = np.concatenate([np.sin(ff), np.cos(ff)], axis=1).T.astype(np.float32)
    expand = np.zeros((P, NBR, P), np.float32)
    for j in range(NBR):
        for c in range(P):
            expand[4 * j + c // 32, j, c] = expand[E + 4 * j + c // 32, j, c] = 1
    return {"cos": np.concatenate([cos, cos]), "sin": np.concatenate([sin, sin]), "four": four,
            "expand": expand, "eye": np.eye(P, dtype=np.float32)}


def kernel(**inputs):
    import numpy as _np
    import concourse.bacc as _bacc
    from concourse import mybir as _mybir
    from concourse.bass_utils import run_bass_kernel_spmd as _run

    i = {k.removeprefix("L0_"): _np.asarray(v) for k, v in inputs.items()}
    swap = _np.concatenate([_np.arange(1, DH, 2), _np.arange(0, DH, 2)])
    w = i["attn_w_qkv"].reshape(3, H, DH, D)
    w_head = _np.concatenate([w[0], w[1], w[0][:, swap], w[1][:, swap], w[2]], axis=1).transpose(0, 2, 1)
    w1 = _np.concatenate([i["ffn_w1"].transpose(1, 0, 2).reshape(D, -1), i["ffn_sw1"].transpose(1, 0, 2).reshape(D, -1)], axis=1)
    b1 = _np.concatenate([i["ffn_b1"].reshape(-1), i["ffn_sb1"].reshape(-1)]).reshape(NB, P).T
    w2 = _np.concatenate([i["ffn_w2"].reshape(-1, D), i["ffn_sw2"].reshape(-1, D)]).reshape(NB, P, D).transpose(1, 0, 2)
    wf = i["attn_w_fproj"].T
    bf = i["attn_b_fproj"][:, None]
    c = constants()
    arrays = {
        "x": i["attn_x"], "w_head": w_head, "wv_all": i["attn_w_qkv"][2 * H * DH:].reshape(P, -1),
        "wf": _np.concatenate([wf, wf], axis=1), "bf": _np.concatenate([bf, bf]), "four": c["four"],
        "cos": c["cos"], "sin": c["sin"], "w_out": i["attn_w_out"].T.reshape(PAIRS, P, D),
        "b_out": _np.tile(i["attn_b_out"], (P, 1)), "rw": i["ffn_router_w"],
        "rb": _np.tile(i["ffn_router_b"], (P, 1)), "w1": w1, "b1": b1, "w2": w2,
        "b2": _np.concatenate([i["ffn_b2"], i["ffn_b2"]]), "sb2": i["ffn_sb2"].T, "expand": c["expand"], "eye": c["eye"],
    }
    arrays = {k: _np.ascontiguousarray(v) for k, v in arrays.items()}
    nc = _bacc.Bacc("TRN2", target_bir_lowering=False, num_devices=1)
    args = [nc.dram_tensor(k, v.shape, _mybir.dt.from_np(v.dtype), kind="ExternalInput").ap() for k, v in arrays.items()]
    args.append(nc.dram_tensor("out", (1, N, D), _mybir.dt.float32, kind="ExternalOutput").ap())
    program(nc, *args)
    r = _run(nc, [arrays], core_ids=[0])
    return r.results[0]["out"]
```

```python
from contextlib import ExitStack

import numpy as np

import concourse.bass as bass
from concourse import mybir

F32 = mybir.dt.float32
F32R = mybir.dt.float32r
F16 = mybir.dt.float16
U32 = mybir.dt.uint32
ALU = mybir.AluOpType
ACT = mybir.ActivationFunctionType
AX = mybir.AxisListType
RMAX = bass.bass_isa.ReduceOp.absmax

P = 128
N = 2048
D = 128
NT = N // P
H = 16
DH = 64
PAIRS = H // 2
QC = 512
NQ = N // QC
QT = QC // P
STEPS = N // (2 * P)
UNITS = 2 * NQ
PAIR_STEPS = UNITS * STEPS
PF = 4
KC = N // 512
LEAD = 3
WCOLS = 5 * DH
E = 64
TOPK = 8
HID = 2560
NB = HID // P
NBR = 2048 // P
EPS = 1e-5
SCALE = DH ** -0.5
VW = 2 * DH + 2
OW = 2 * DH + 1
DMA = 16
MOVES = 18
MAX_AT = 2
PROJ_AT = (0, 3, 7, 9)
ROT_AT = (1, 5, 8, 11)
V_AT = (15, 23)
SPLIT_AT = 24


def dve_low(L):
    return 512 if 2 <= L % (NQ * STEPS) < 17 else 384


def items(U, s, last):
    out = []
    qc, a = U % NQ, (U // NQ) % 2
    sl = STEPS * qc + s
    M, m = (U + 2, s - MAX_AT) if s >= MAX_AT else (U + 1, s - MAX_AT + STEPS)
    if not (last and M >= UNITS):
        out += [("max", M, i // KC, i % KC) for i in (2 * m, 2 * m + 1)]
    if s == MAX_AT and not (last and U + 1 >= UNITS):
        out.append(("turn_max", U + 1))
    if not (last and a == 1):
        for kind, steps in (("proj", PROJ_AT), ("rot", ROT_AT), ("v", V_AT)):
            if sl in steps:
                out.append((kind, steps.index(sl)))
    if U > NQ and s == 4:
        out.append(("turn_o", (U - 1) % NQ))
    if U > NQ and s == 6:
        out.append(("out_proj", (U - 1) % NQ))
    return out


def head_items():
    return [(k, c) for c in range(4) for k in ("proj", "rot")] + [("v", 0), ("v", 1)]


def max_items(U):
    return [("max", U, i // KC, i % KC) for i in range(QT * KC)]


PRE = head_items() + max_items(0) + [("turn_max", 0)] + max_items(1)[:2 * (STEPS - MAX_AT)]
A1 = len(PRE) + sum(len(items(0, s, False)) for s in range(STEPS))
AP = sum(len(items(U, s, False)) for U in range(1, UNITS + 1) for s in range(STEPS))


def program(nc, x, w_head, wqkv_all, wf, bf, four, cos, sin, w_out, b_out, rw, rb, w1, b1, w2, b2, sb2,
            expand, eye, out):
    ctx = ExitStack()
    with ctx:
        def sb(name, shape, dt, where=ctx):
            return where.enter_context(nc.sbuf_tensor(name, shape, dt))

        def sem(name):
            return ctx.enter_context(nc.semaphore(name))

        gate = sb("gate", [P, NT, D], F32)
        xh16 = sb("xh16", [P, N], F16)
        xl16 = sb("xl16", [P, N], F16)
        cos_sb = sb("cos_sb", [P, N], F32)
        sin_sb = sb("sin_sb", [P, N], F32)
        fenc = sb("fenc", [P, N], F32)
        eye_sb = sb("eye_sb", [P, P], F32)
        bout_sb = sb("bout_sb", [P, D], F32)
        wmax = sb("wmax", [P, 4], F32)
        early = ExitStack()
        x_sb = sb("x_sb", [P, NT, D], F32, early)
        xn = sb("xn", [P, NT, D], F32, early)
        x_hi = sb("x_hi", [P, N], F32R, early)
        x_lo = sb("x_lo", [P, N], F32R, early)
        stats = sb("stats", [P, NT, 6], F32, early)
        mv = sb("mv", [P, NT, 2], F32, early)
        rs = sb("rs", [P, 4, NT], F32, early)
        wqkv_sb = sb("wqkv_sb", [P, 3 * H * DH], F32, early)
        four_sb = sb("four_sb", [32, N], F32, early)
        wf_sb = sb("wf_sb", [32, P], F32, early)
        bf_sb = sb("bf_sb", [P, 1], F32, early)
        rw_sb = sb("rw_sb", [P, E], F32, early)
        rw_hi = sb("rw_hi", [P, E], F32R, early)
        rw_lo = sb("rw_lo", [P, E], F32R, early)
        rb_sb = sb("rb_sb", [P, E], F32, early)
        logit = sb("logit", [P, NT, E], F32, early)
        prob = sb("prob", [P, NT, E], F32, early)
        rest = sb("rest", [P, NT, E], F32, early)
        top = sb("top", [P, NT, TOPK], F32, early)
        rstat = sb("rstat", [P, 5, NT], F32, early)
        cwt = sb("cwt", [P, NT, 2, E], F32, early)
        cw = sb("cw", [P, N], F32R, early)
        ex_in = sb("ex_in", [P, NBR, P], F32, early)
        ex = sb("ex", [P, NBR, P], F32R, early)
        w1_sb = sb("w1_sb", [P, HID], F32, early)
        w1_hi = sb("w1_hi", [P, HID], F32R, early)
        w1_lo = sb("w1_lo", [P, HID], F32R, early)
        b1_sb = sb("b1_sb", [P, NB], F32, early)
        w2_sb = sb("w2_sb", [P, NB, D], F32, early)
        b2_sb = sb("b2_sb", [P, D], F32, early)
        b2_hi = sb("b2_hi", [P, D], F32R, early)
        b2_lo = sb("b2_lo", [P, D], F32R, early)
        sb2_sb = sb("sb2_sb", [P, 2], F32, early)
        sb2_sum = sb("sb2_sum", [P, 1], F32, early)
        act_h = sb("act_h", [P, 2, 512], F32, early)
        hid = sb("hid", [P, 2, 512], F32, early)
        gate_t = sb("gate_t", [P, 512], F32, early)
        early.close()
        qm1 = [sb(f"qm1_{a}", [P, N], F32R) for a in range(2)]
        km1 = [sb(f"km1_{a}", [P, N], F32R) for a in range(2)]
        qm2 = [sb(f"qm2_{a}", [P, N], F32R) for a in range(2)]
        km2 = [sb(f"km2_{a}", [P, N], F32R) for a in range(2)]
        turn1 = sb("turn1", [P, 2, 512], F32)
        turn2 = sb("turn2", [P, 2, 512], F32)
        qk_hi = sb("qk_hi", [P, N], F32R)
        qk_lo = sb("qk_lo", [P, N], F32R)
        v_sb = [sb(f"v_{a}", [P, NT, VW], F16) for a in range(2)]
        w_in = sb("w_in", [P, WCOLS], F32)
        w_hi = sb("w_hi", [P, WCOLS], F16)
        w_lo = sb("w_lo", [P, WCOLS], F16)
        wo_sb = sb("wo_sb", [P, D], F32)
        pf = sb("pf", [P, PF, 2 * QC], F32)
        ph = sb("ph", [P, 4, 2 * QC], F16)
        pl = sb("pl", [P, 4, 2 * QC], F16)
        max_p = sb("max_p", [P, 2, QT, KC], F32)
        max_n = sb("max_n", [P, 2, QT], F32)
        max_r = sb("max_r", [QT, 2, 2, P], F32R)
        o_raw = sb("o_raw", [P, 2, QT, OW], F32)
        o_sum = sb("o_sum", [P, QT, DH], F32)
        o_rec = sb("o_rec", [P, 2, QT], F32)
        o_sb = sb("o_sb", [P, NT, 2 * DH], F32)
        ot_sb = sb("ot_sb", [P, QC], F32)
        s_acc = sb("s_acc", [P, NT, D], F32)

        ps_s = ctx.enter_context(nc.psum_tensor("ps_s", [P, 2, 2, 512], F32))
        ps_a = ctx.enter_context(nc.psum_tensor("ps_a", [P, 2, 512], F32))
        ps_o = ctx.enter_context(nc.psum_tensor("ps_o", [P, 2, 512], F32))

        ld_again = sem("ld_again")
        ld_x, ld_mlp, ld_pos = sem("ld_x"), sem("ld_mlp"), sem("ld_pos")
        dve_seq = sem("dve_seq")
        var_ready, std_ready = sem("var_ready"), sem("std_ready")
        xn_ready, xt_ready, x_split = sem("xn_ready"), sem("xt_ready"), sem("x_split")
        fenc_ready = sem("fenc_ready")
        wmax_ready, wvall_ready = sem("wmax_ready"), sem("wvall_ready")
        logit_ready, shifted, exps = sem("logit_ready"), sem("shifted"), sem("exps")
        cw_tok, cw_turned, cw_ready = sem("cw_tok"), sem("cw_turned"), sem("cw_ready")
        h_ready, c_ready, sil_ready = sem("h_ready"), sem("c_ready"), sem("sil_ready")
        hid_ready, y_done = sem("hid_ready"), sem("y_done")
        gate_sil, gate_turned, gate_done = sem("gate_sil"), sem("gate_turned"), sem("gate_done")
        w_loaded, w_high, w_split = sem("w_loaded"), sem("w_high"), sem("w_split")
        wo_loaded = sem("wo_loaded")
        aux_ready, aux_free = sem("aux_ready"), sem("aux_free")
        v_high = sem("v_high")
        rope_a, rope_sum, hi_done, lo_done = sem("rope_a"), sem("rope_sum"), sem("hi_done"), sem("lo_done")
        moved, max_ready, max_high, max_rows = sem("moved"), sem("max_ready"), sem("max_high"), sem("max_rows")
        s_ready, probs_ready = sem("s_ready"), sem("probs_ready")
        pl_dve, pl_pool = sem("pl_dve"), sem("pl_pool")
        pv_done, acc_copied = sem("pv_done"), sem("acc_copied")
        rec_ready, osum_ready, o_ready = sem("rec_ready"), sem("osum_ready"), sem("o_ready")
        const_ready, fin, stored = sem("const_ready"), sem("fin"), sem("stored")

        MLP_LOADS = 13
        x_again = pf[:, 0:2, :].rearrange("p a (t d) -> p (a t) d", d=D)
        out_v = out[0].rearrange("(t p) d -> p t d", p=P)
        block = ctx.enter_context(nc.Block())

        @block.sync
        def _(sp):
            sp.dma_start(x_sb[:], x[0].rearrange("(t p) d -> p t d", p=P)).then_inc(ld_x, DMA)
            sp.dma_start(eye_sb[:], eye).then_inc(ld_x, DMA)
            for dst, src in ((rw_sb, rw), (rb_sb, rb), (wf_sb, wf), (bf_sb, bf), (four_sb, four),
                             (wqkv_sb, wqkv_all), (w1_sb, w1), (b1_sb, b1), (ex_in, expand), (w2_sb, w2),
                             (b2_sb, b2), (sb2_sb, sb2), (bout_sb, b_out)):
                sp.dma_start(dst[:], src).then_inc(ld_mlp, DMA)
            sp.dma_start(cos_sb[:], cos).then_inc(ld_pos, DMA)
            sp.dma_start(sin_sb[:], sin).then_inc(ld_pos, DMA)
            sp.wait_ge(gate_done, 4)
            sp.dma_start(w_in[:], w_head[0]).then_inc(w_loaded, DMA)

            def move(first, end, a, chunks):
                sp.wait_ge(lo_done, chunks + end)
                c = slice(first * 512, end * 512)
                for dst, src, p0 in ((qm1[a][0:DH, c], qk_hi, 0), (qm1[a][DH:P, c], qk_lo, 0),
                                     (km1[a][0:DH, c], qk_hi, DH), (km1[a][DH:P, c], qk_hi, DH),
                                     (qm2[a][0:DH, c], qk_hi, 0), (km2[a][0:DH, c], qk_lo, DH)):
                    sp.dma_start(dst.bitcast(F32), src[p0:p0 + DH, c].bitcast(F32)).then_inc(moved, DMA)

            def max_row(U, consumed):
                a, qc = (U // NQ) % 2, U % NQ
                sp.wait_ge(aux_free, consumed)
                for part in range(2):
                    sp.dma_start(qm2[a][DH + part:DH + part + 1, qc * QC:(qc + 1) * QC].bitcast(F32)
                                 .rearrange("o (t q) -> o t q", t=QT),
                                 max_r[:, U % 2, part, :].bitcast(F32)).then_inc(max_rows, DMA)

            def unit(U, g, k, last):
                qc, hd = U % NQ, U // NQ
                a = hd % 2
                if U == 1:
                    sp.wait_ge(aux_ready, k + AP * g)
                    sp.dma_start(wo_sb[:], w_out[g]).then_inc(wo_loaded, DMA)
                for s in range(STEPS):
                    for it in items(U, s, last):
                        k += 1
                        if it[0] == "turn_max":
                            max_row(it[1], k + AP * g)
                    if qc == 1 and s == MAX_AT and not (last and a == 1):
                        for first, end in ((0, 2), (2, 3), (3, 4)):
                            move(first, end, 1 - a, 4 * (hd + 1) + 8 * g)
                if qc == 1 and not last:
                    sp.wait_ge(w_split, hd + 2 + 2 * g)
                    sp.dma_start(w_in[:], w_head[g * 2 + (hd + 2)]).then_inc(w_loaded, DMA)
                return k

            move(0, 2, 0, 0)
            move(2, 3, 0, 0)
            move(3, 4, 0, 0)
            sp.wait_ge(w_split, 1)
            sp.dma_start(w_in[:], w_head[1]).then_inc(w_loaded, DMA)
            k = 0
            for it in PRE:
                k += 1
                if it[0] == "turn_max":
                    max_row(0, k)
            k = unit(0, 0, k, False)
            with sp.Fori(0, PAIRS - 1) as g:
                kk = k
                for U in range(1, UNITS + 1):
                    kk = unit(U, g, kk, False)
            for U in range(1, UNITS):
                k = unit(U, PAIRS - 1, k, True)
            sp.wait_ge(pl_dve, PAIRS * PAIR_STEPS)
            sp.wait_ge(pl_pool, PAIRS * PAIR_STEPS)
            sp.dma_start(x_again, x[0].rearrange("(t p) d -> p t d", p=P)).then_inc(ld_again, DMA)
            for c in range(NQ):
                sp.wait_ge(fin, c + 1)
                sp.dma_start(out_v[:, QT * c:QT * c + QT, :], o_sb[:, QT * c:QT * c + QT, :]).then_inc(stored, DMA)
            sp.wait_ge(stored, NQ * DMA)

        @block.tensor
        def _(pe):
            mm = nc.tensor.matmul

            def mm3(dst, s_hi, s_lo, m_hi, m_lo, start=True, stop=True):
                mm(dst, s_hi, m_hi, start=start, stop=False)
                mm(dst, s_lo, m_hi, start=False, stop=False)
                return mm(dst, s_hi, m_lo, start=False, stop=stop)

            pe.wait_ge(ld_x, 2 * DMA)
            for c in range(4):
                pe.wait_ge(xn_ready, c + 1)
                for i in range(4):
                    last = nc.tensor.transpose(ps_s[:, c // 2, c % 2, i * P:(i + 1) * P], xn[:, 4 * c + i, :], eye_sb[:])
                last.then_inc(xt_ready, 1)
            pe.wait_ge(x_split, 4)
            pe.wait_ge(ld_mlp, MLP_LOADS * DMA)
            for c in range(4):
                mm(ps_s[:, c // 2, c % 2, :], wf_sb[:], four_sb[:, c * 512:(c + 1) * 512], start=True, stop=True)\
                    .then_inc(fenc_ready, 1)
            pe.wait_ge(dve_seq, 1)
            for i in range(NT):
                dst = ps_o[:, i // 8, (i % 8) * E:(i % 8 + 1) * E]
                t = slice(i * P, (i + 1) * P)
                mm3(dst, x_hi[:, t], x_lo[:, t], rw_hi[:], rw_lo[:], stop=False)
                last = mm(dst, x_lo[:, t], rw_lo[:], start=False, stop=True)
            last.then_inc(logit_ready, 1)
            pe.wait_ge(cw_tok, 1)
            for c in range(4):
                if c >= 2:
                    pe.wait_ge(cw_ready, c - 1)
                for i in range(4):
                    last = nc.tensor.transpose(ps_a[:, c % 2, i * P:(i + 1) * P], cwt[:, 4 * c + i, :, :], eye_sb[:])
                last.then_inc(cw_turned, 1)
            pe.wait_ge(cw_ready, 4)

            with pe.Fori(0, 4) as tc:
                tok = bass.ts(tc, 512)

                def down(j):
                    if j < NBR:
                        pe.wait_ge(hid_ready, tc * NBR + (j + 1))
                    else:
                        pe.wait_ge(sil_ready, tc * NB + (j + 1))
                    mm(ps_o[:, 0, :], w2_sb[:, j, :], hid[:, j % 2, :], start=False, stop=(j == NB - 1))\
                        .then_inc(y_done, 1)

                mm(ps_o[:, 0, :], b2_hi[:], cw[:, tok], start=True, stop=False)
                mm(ps_o[:, 0, :], b2_lo[:], cw[:, tok], start=False, stop=False)
                for j in range(NB):
                    if j >= 2:
                        pe.wait_ge(sil_ready, tc * NB + (j - 1))
                    c = slice(j * P, (j + 1) * P)
                    mm3(ps_s[:, j % 2, 0, :], w1_hi[:, c], w1_lo[:, c], x_hi[:, tok], x_lo[:, tok]).then_inc(h_ready, 1)
                    if j < NBR:
                        mm(ps_s[:, j % 2, 1, :], ex[:, j, :], cw[:, tok], start=True, stop=True).then_inc(c_ready, 1)
                    if j >= 1:
                        down(j - 1)
                down(NB - 1)
                pe.wait_ge(gate_sil, tc + 1)
                for i in range(4):
                    last = nc.tensor.transpose(ps_a[:, 0, i * P:(i + 1) * P], gate_t[:, i * P:(i + 1) * P], eye_sb[:])
                last.then_inc(gate_turned, 1)

            pe.wait_ge(gate_done, 4)

            def aux(it, k, g, hn, wo_count, turned):
                kind, bank = it[0], k % 2
                dst = ps_a[:, bank, :]
                if k >= 2:
                    pe.wait_ge(aux_free, k - 1 + AP * g)
                if kind == "max":
                    _, U, qt, kc = it
                    a, qc = (U // NQ) % 2, U % NQ
                    if qc == 0 and qt == 0 and kc == 0:
                        pe.wait_ge(moved, DMA * MOVES * (U // NQ + 1) + 2 * DMA * MOVES * g)
                    q0 = qc * QC + qt * P
                    last = mm(dst, qm1[a][:, q0:q0 + P], km1[a][:, kc * 512:(kc + 1) * 512], start=True, stop=True)
                elif kind == "turn_max":
                    U = it[1]
                    pe.wait_ge(max_ready, U + 1 + UNITS * g)
                    last = mm(ps_a[0:QT, bank, 0:P], max_n[:, U % 2, :], eye_sb[:], start=True, stop=True)
                elif kind in ("proj", "rot"):
                    if it == ("proj", 0):
                        pe.wait_ge(w_split, hn + 1)
                    w = slice(0, P) if kind == "proj" else slice(P, 2 * P)
                    t = slice(it[1] * 512, (it[1] + 1) * 512)
                    last = mm3(dst, w_hi[:, w], w_lo[:, w], xh16[:, t], xl16[:, t])
                elif kind == "v":
                    for i in range(8):
                        t = slice((8 * it[1] + i) * P, (8 * it[1] + i + 1) * P)
                        last = mm3(dst[:, i * DH:(i + 1) * DH], xh16[:, t], xl16[:, t], w_hi[:, 2 * P:], w_lo[:, 2 * P:])
                elif kind == "turn_o":
                    pe.wait_ge(o_ready, NQ + it[1] + 1 + UNITS * g)
                    for i in range(QT):
                        last = nc.tensor.transpose(dst[:, i * P:(i + 1) * P], o_sb[:, QT * it[1] + i, :], eye_sb[:])
                else:
                    pe.wait_ge(aux_free, turned + AP * g)
                    pe.wait_ge(wo_loaded, wo_count)
                    for i in range(QT):
                        last = mm(dst[:, i * P:(i + 1) * P], ot_sb[:, i * P:(i + 1) * P], wo_sb[:], start=True, stop=True)
                last.then_inc(aux_ready, 1)

            def scores(L, i, g):
                U = L // STEPS
                a, qc = (U // NQ) % 2, U % NQ
                if L % STEPS == 0 and i == 0:
                    if qc == 0:
                        pe.wait_ge(moved, DMA * MOVES * (U // NQ + 1) + 2 * DMA * MOVES * g)
                    pe.wait_ge(max_rows, 2 * DMA * (U + 1) + 2 * DMA * UNITS * g)
                if L >= 2 and i == 0:
                    pe.wait_ge(probs_ready, L - 1 + PAIR_STEPS * g)
                q = slice(qc * QC, (qc + 1) * QC)
                kt = slice((2 * (L % STEPS) + i) * P, (2 * (L % STEPS) + i + 1) * P)
                mm(ps_s[:, L % 2, i, :], km1[a][:, kt], qm1[a][:, q], start=True, stop=False)
                last = mm(ps_s[:, L % 2, i, :], km2[a][0:DH + 2, kt], qm2[a][0:DH + 2, q], start=False, stop=True)
                if i == 1:
                    last.then_inc(s_ready, 1)

            def times_v(L, n, g):
                U = L // STEPS
                a = (U // NQ) % 2
                if n == 0:
                    if L % STEPS == 0 and not (isinstance(g, int) and U + UNITS * g == 0):
                        pe.wait_ge(acc_copied, U + UNITS * g)
                    pe.wait_ge(pl_dve, L + 1 + PAIR_STEPS * g)
                if n == dve_low(L) // P:
                    pe.wait_ge(pl_pool, L + 1 + PAIR_STEPS * g)
                i, qt = n // QT, n % QT
                kt = 2 * (L % STEPS) + i
                dst = ps_o[:, qt // 2, (qt % 2) * 256:(qt % 2) * 256 + OW]
                c = slice(i * QC + qt * P, i * QC + (qt + 1) * P)
                mm(dst, ph[:, L % 4, c], v_sb[a][:, kt, 0:OW], start=(kt == 0 and qt % 2 == 0),
                   stop=False, skip_group_check=True)
                last = mm(dst[:, 0:DH + 1], pl[:, L % 4, c], v_sb[a][:, kt, 0:DH + 1], start=False,
                          stop=(kt == NT - 1), skip_group_check=True)
                if n == 2 * QT - 1:
                    last.then_inc(pv_done, 1)

            def unit(U, g, k, last):
                turned = 0
                for s in range(STEPS):
                    L = U * STEPS + s
                    work, n = items(U, s, last), 0
                    parts = [(times_v, L, i) for i in range(2 * QT)]
                    if not (last and L + LEAD >= PAIR_STEPS):
                        parts = [(scores, L + LEAD, i) for i in range(2)] + parts
                    for what, step, i in parts:
                        what(step, i, g)
                        if n < len(work) and (what is scores or (what is times_v and i in (2, 5))):
                            aux(work[n], k, g, U // NQ + 1 + 2 * g, DMA * (g + 1), turned)
                            k, n = k + 1, n + 1
                            if work[n - 1][0] == "turn_o":
                                turned = k
                    assert n == len(work)
                return k

            k = 0
            for it in PRE:
                aux(it, k, 0, 0, 0, 0)
                k += 1
            pe.wait_ge(const_ready, 4)
            for L in range(LEAD):
                scores(L, 0, 0)
                scores(L, 1, 0)
            k = unit(0, 0, k, False)
            with pe.Fori(0, PAIRS - 1) as g:
                kk = k
                for U in range(1, UNITS + 1):
                    kk = unit(U, g, kk, False)
            for U in range(1, UNITS):
                k = unit(U, PAIRS - 1, k, True)
            for it in (("turn_o", NQ - 1), ("out_proj", NQ - 1)):
                aux(it, k, PAIRS - 1, 0, DMA * PAIRS, k)
                k += 1

        @block.scalar
        def _(act):
            act.wait_ge(var_ready, 1)
            nc.scalar.activation(rs[:, 1, :], rs[:, 0, :], ACT.Sqrt).then_inc(std_ready, 1)
            act.wait_ge(shifted, 1)
            nc.scalar.activation(prob[:], logit[:], ACT.Exp).then_inc(exps, 1)
            act.wait_ge(cw_ready, 4)
            with act.Fori(0, 4) as tc:
                for j in range(NB):
                    act.wait_ge(h_ready, tc * NB + (j + 1))
                    if j < NBR:
                        if j >= 2:
                            act.wait_ge(hid_ready, tc * NBR + (j - 1))
                        dst = act_h[:, j % 2, :]
                    else:
                        act.wait_ge(y_done, tc * NB + (j - 1))
                        dst = hid[:, j % 2, :]
                    nc.scalar.activation(dst, ps_s[:, j % 2, 0, :], ACT.Silu, bias=b1_sb[:, j:j + 1]).then_inc(sil_ready, 1)
                act.wait_ge(y_done, tc * NB + NB)
                nc.scalar.activation(gate_t[:], ps_o[:, 0, :], ACT.Silu, bias=sb2_sum[:, 0:1]).then_inc(gate_sil, 1)
            act.wait_ge(gate_done, 4)

            def exp_step(L, g):
                act.wait_ge(s_ready, L + 1 + PAIR_STEPS * g)
                if L >= PF:
                    act.wait_ge(pl_dve, L - PF + 1 + PAIR_STEPS * g)
                    act.wait_ge(pl_pool, L - PF + 1 + PAIR_STEPS * g)
                if L >= 4:
                    act.wait_ge(pv_done, L - 3 + PAIR_STEPS * g)
                nc.scalar.activation(pf[:, L % PF, :].rearrange("p (i q) -> p i q", i=2), ps_s[:, L % 2, :, :],
                                     ACT.Exp, scale=SCALE)
                nc.scalar.activation(ph[:, L % 4, :].rearrange("p (i q) -> p i q", i=2), ps_s[:, L % 2, :, :],
                                     ACT.Exp, scale=SCALE).then_inc(probs_ready, 1)

            def high_part(c, hn, first):
                if c == 0 and not first:
                    act.wait_ge(moved, DMA * MOVES * hn)
                act.wait_ge(rope_sum, 4 * hn + c + 1)
                nc.scalar.activation(qk_hi[:, c * 512:(c + 1) * 512], turn1[:, c % 2, :], ACT.Copy).then_inc(hi_done, 1)

            def take_sums(U, g):
                act.wait_ge(pv_done, STEPS * U + PAIR_STEPS * g)
                nc.scalar.activation(o_raw[:, (U - 1) % 2, :, :].rearrange("p (b i) c -> p b i c", b=2),
                                     ps_o[:].rearrange("p b (i c) -> p b i c", i=2)[:, :, :, 0:OW],
                                     ACT.Copy).then_inc(acc_copied, 1)

            def unit(U, g, last):
                for s in range(STEPS):
                    L = U * STEPS + s
                    if s == 0 and not (isinstance(g, int) and U + UNITS * g == 0):
                        take_sums(U, g)
                    if not (last and L + LEAD >= PAIR_STEPS):
                        exp_step(L + LEAD, g)
                    sl = STEPS * (U % NQ) + s
                    if sl - 2 in ROT_AT and not (last and U // NQ == 1):
                        high_part(ROT_AT.index(sl - 2), U // NQ + 1 + 2 * g, False)

            for c in range(4):
                high_part(c, 0, True)
            for L in range(LEAD):
                exp_step(L, 0)
            unit(0, 0, False)
            with act.Fori(0, PAIRS - 1) as g:
                for U in range(1, UNITS + 1):
                    unit(U, g, False)
            for U in range(1, UNITS):
                unit(U, PAIRS - 1, True)
            take_sums(UNITS, PAIRS - 1)

        @block.vector
        def _(dve):
            V = nc.vector
            seq = [0]

            def link(ins):
                seq[0] += 1
                ins.then_inc(dve_seq, 1)
                dve.wait_ge(dve_seq, seq[0])

            dve.wait_ge(ld_mlp, MLP_LOADS * DMA)
            V.tensor_copy(rw_hi[:], rw_sb[:]).then_inc(w_high, 1)
            dve.wait_ge(w_high, 1)
            link(V.tensor_tensor(rw_lo[:], rw_sb[:], rw_hi[:].bitcast(F32), ALU.subtract))
            dve.wait_ge(ld_x, 2 * DMA)
            for i in range(NT):
                st = V.bn_stats(stats[:, i, :], x_sb[:, i, :])
            link(st)
            for i in range(NT):
                st = V.bn_aggr(mv[:, i, :], stats[:, i, :])
            link(st)
            V.tensor_scalar(rs[:, 0, :], mv[:, :, 1], EPS, None, ALU.add).then_inc(var_ready, 1)
            dve.wait_ge(std_ready, 1)
            link(V.reciprocal(rs[:, 2, :], rs[:, 1, :]))
            link(V.tensor_tensor(rs[:, 3, :], rs[:, 2, :], rs[:, 2, :], ALU.mult))
            link(V.tensor_tensor(rs[:, 1, :], rs[:, 3, :], rs[:, 0, :], ALU.mult))
            link(V.tensor_scalar(rs[:, 3, :], rs[:, 1, :], -0.5, 1.5, ALU.mult, ALU.add))
            link(V.tensor_tensor(rs[:, 1, :], rs[:, 3, :], rs[:, 2, :], ALU.mult))
            for i in range(NT):
                ins = V.tensor_scalar(xn[:, i, :], x_sb[:, i, :], mv[:, i, 0:1], rs[:, 1, i:i + 1], ALU.subtract, ALU.mult)
                if i % 4 == 3:
                    ins.then_inc(xn_ready, 1)
            for c in range(4):
                dve.wait_ge(xt_ready, c + 1)
                t = slice(c * 512, (c + 1) * 512)
                link(V.tensor_copy(x_hi[:, t], ps_s[:, c // 2, c % 2, :]))
                V.tensor_tensor(x_lo[:, t], ps_s[:, c // 2, c % 2, :], x_hi[:, t].bitcast(F32), ALU.subtract)
                link(V.tensor_copy(xh16[:, t], ps_s[:, c // 2, c % 2, :]))
                V.tensor_tensor(xl16[:, t], ps_s[:, c // 2, c % 2, :], xh16[:, t], ALU.subtract).then_inc(x_split, 1)
            link(V.tensor_copy(w1_hi[:], w1_sb[:]))
            V.tensor_tensor(w1_lo[:], w1_sb[:], w1_hi[:].bitcast(F32), ALU.subtract)
            V.tensor_copy(ex[:], ex_in[:])
            link(V.tensor_copy(b2_hi[:], b2_sb[:]))
            V.tensor_tensor(b2_lo[:], b2_sb[:], b2_hi[:].bitcast(F32), ALU.subtract)
            V.tensor_tensor(sb2_sum[:], sb2_sb[:, 0:1], sb2_sb[:, 1:2], ALU.add)
            for c in range(4):
                dve.wait_ge(fenc_ready, c + 1)
                V.tensor_scalar(fenc[:, c * 512:(c + 1) * 512], ps_s[:, c // 2, c % 2, :], bf_sb[:, 0:1], None, ALU.add)
            V.tensor_reduce(wmax[:, 0:1], wqkv_sb[:], AX.X, ALU.max, apply_absolute_value=True).then_inc(wmax_ready, 1)
            dve.wait_ge(logit_ready, 1)
            for b in range(2):
                ins = V.tensor_tensor(logit[:, 8 * b:8 * b + 8, :], ps_o[:, b, :].rearrange("p (t e) -> p t e", t=8),
                                      rb_sb[:].unsqueeze(1).to_broadcast([P, 8, E]), ALU.add)
            link(ins)
            link(V.tensor_reduce(rstat[:, 0, :], logit[:], AX.X, ALU.max))
            V.tensor_tensor(logit[:], logit[:], rstat[:, 0, :].unsqueeze(2).to_broadcast([P, NT, E]), ALU.subtract)\
                .then_inc(shifted, 1)
            dve.wait_ge(exps, 1)
            link(V.tensor_reduce(rstat[:, 1, :], prob[:], AX.X, ALU.add))
            link(V.reciprocal(rstat[:, 2, :], rstat[:, 1, :]))
            link(V.tensor_tensor(prob[:], prob[:], rstat[:, 2, :].unsqueeze(2).to_broadcast([P, NT, E]), ALU.mult))
            for i in range(NT):
                ins = V.max(top[:, i, :], prob[:, i, :])
            link(ins)
            for i in range(NT):
                ins = V.match_replace(rest[:, i, :], top[:, i, :], prob[:, i, :], 0.0)
            link(ins)
            V.tensor_tensor(logit[:], prob[:], rest[:], ALU.subtract)
            link(V.tensor_reduce(rstat[:, 3, :], top[:], AX.X, ALU.add))
            link(V.reciprocal(rstat[:, 4, :], rstat[:, 3, :]))
            for i in range(2):
                ins = V.tensor_tensor(cwt[:, :, i, :], logit[:], rstat[:, 4, :].unsqueeze(2).to_broadcast([P, NT, E]), ALU.mult)
            ins.then_inc(cw_tok, 1)
            for c in range(4):
                dve.wait_ge(cw_turned, c + 1)
                t = slice(c * 512, (c + 1) * 512)
                link(V.tensor_copy(cw[:, t], ps_a[:, c % 2, :]))
                V.tensor_tensor(cw[E:, t], ps_a[E:, c % 2, :], cw[E:, t].bitcast(F32), ALU.subtract).then_inc(cw_ready, 1)

            with dve.Fori(0, 4) as tc:
                for j in range(NBR):
                    dve.wait_ge(sil_ready, tc * NB + (j + 1))
                    dve.wait_ge(c_ready, tc * NBR + (j + 1))
                    if j >= 2:
                        dve.wait_ge(y_done, tc * NB + (j - 1))
                    V.tensor_tensor(hid[:, j % 2, :], ps_s[:, j % 2, 1, :], act_h[:, j % 2, :], ALU.mult)\
                        .then_inc(hid_ready, 1)
                dve.wait_ge(gate_turned, tc + 1)
                V.tensor_copy(gate[:, bass.ts(tc, 4), :], ps_a[:, 0, :].rearrange("p (t d) -> p t d", t=4))\
                    .then_inc(gate_done, 1)

            dve.wait_ge(gate_done, 4)
            dve.wait_ge(ld_pos, 2 * DMA)
            dve.wait_ge(wvall_ready, 1)
            link(V.tensor_scalar(wmax[:, 2:3], wmax[:, 1:2], 2.0 ** -100, None, ALU.max))
            link(V.tensor_single_scalar(wmax[:, 2:3].bitcast(U32), wmax[:, 2:3].bitcast(U32), 0x7F800000, ALU.bitwise_and))
            link(V.reciprocal(wmax[:, 3:4], wmax[:, 2:3]))
            link(V.memset(s_acc[:], 0.0))

            def split_weights(hn):
                dve.wait_ge(w_loaded, DMA * (hn + 1))
                V.tensor_scalar(w_hi[:], w_in[:], wmax[:, 3:4], None, ALU.mult).then_inc(w_high, 1)
                dve.wait_ge(w_high, hn + 2)
                V.scalar_tensor_tensor(out=w_lo[:], in0=w_in[:], scalar=wmax[:, 3:4], in1=w_hi[:],
                                       op0=ALU.mult, op1=ALU.subtract).then_inc(w_split, 1)

            def combine_max(U, g, k):
                dve.wait_ge(aux_free, k)
                V.tensor_reduce(max_n[:, U % 2, :], max_p[:, U % 2, :, :], AX.X, ALU.max, negate=True).then_inc(max_ready, 1)

            def low_probs(L, g):
                dve.wait_ge(probs_ready, L + 1 + PAIR_STEPS * g)
                c = slice(0, dve_low(L))
                V.tensor_tensor(pl[:, L % 4, c], pf[:, L % PF, c], ph[:, L % 4, c], ALU.subtract).then_inc(pl_dve, 1)

            def aux(it, k, g, hn, first, vpar):
                kind = it[0]
                src = ps_a[:, k % 2, :]
                dve.wait_ge(aux_ready, k + 1 + AP * g)
                if kind == "max":
                    _, U, qt, kc = it
                    V.tensor_reduce(max_p[:, U % 2, qt, kc:kc + 1], src, AX.X, ALU.max).then_inc(aux_free, 1)
                elif kind == "turn_max":
                    U = it[1]
                    if not (isinstance(g, int) and U + UNITS * g < 2):
                        dve.wait_ge(max_rows, 2 * DMA * (U - 1) + 2 * DMA * UNITS * g)
                    src = ps_a[0:QT, k % 2, 0:P]
                    V.tensor_copy(max_r[:, U % 2, 0, :], src).then_inc(max_high, 1)
                    dve.wait_ge(max_high, U + 1 + UNITS * g)
                    V.tensor_tensor(max_r[:, U % 2, 1, :], src, max_r[:, U % 2, 0, :].bitcast(F32), ALU.subtract)\
                        .then_inc(aux_free, 1)
                elif kind == "proj":
                    c = it[1]
                    if not (first and c < 2):
                        dve.wait_ge(lo_done, 4 * hn + (c - 1))
                    V.scalar_tensor_tensor(out=turn1[:, c % 2, :], in0=src, scalar=wmax[:, 2:3],
                                           in1=cos_sb[:, c * 512:(c + 1) * 512], op0=ALU.mult, op1=ALU.mult).then_inc(aux_free, 1)
                elif kind == "rot":
                    c = it[1]
                    V.scalar_tensor_tensor(out=turn2[:, c % 2, :], in0=src, scalar=wmax[:, 2:3],
                                           in1=sin_sb[:, c * 512:(c + 1) * 512], op0=ALU.mult, op1=ALU.mult).then_inc(aux_free, 1)
                elif kind == "v":
                    src = src.rearrange("p (t d) -> p t d", t=8)
                    t = slice(8 * it[1], 8 * it[1] + 8)
                    V.tensor_copy(v_sb[vpar][:, t, 0:DH], src).then_inc(v_high, 1)
                    dve.wait_ge(v_high, 2 * hn + (it[1] + 1))
                    V.tensor_tensor(v_sb[vpar][:, t, DH + 1:OW], src, v_sb[vpar][:, t, 0:DH], ALU.subtract).then_inc(aux_free, 1)
                elif kind == "turn_o":
                    V.tensor_copy(ot_sb[:], src).then_inc(aux_free, 1)
                else:
                    t = slice(QT * it[1], QT * it[1] + QT)
                    V.tensor_tensor(s_acc[:, t, :], src.rearrange("p (t d) -> p t d", t=QT), s_acc[:, t, :], ALU.add)\
                        .then_inc(aux_free, 1)

            def take_rec(U, g):
                dve.wait_ge(acc_copied, U + UNITS * g)
                V.reciprocal(o_rec[:, (U - 1) % 2, :], o_raw[:, (U - 1) % 2, :, DH]).then_inc(rec_ready, 1)

            def unit(U, g, k, last):
                hd = U // NQ
                hn = hd + 1 + 2 * g
                for s in range(STEPS):
                    L = U * STEPS + s
                    sl = STEPS * (U % NQ) + s
                    if s == MAX_AT and not (last and U + 1 >= UNITS):
                        combine_max(U + 1, g, k + AP * g)
                    Ln = L + LEAD - 1
                    work = items(U, s, last)
                    for n, it in enumerate(work):
                        aux(it, k, g, hn, False, 1 - hd % 2)
                        k += 1
                        if n == 0 and not (last and Ln >= PAIR_STEPS):
                            low_probs(Ln, g)
                    if not work and not (last and Ln >= PAIR_STEPS):
                        low_probs(Ln, g)
                    if s == 1 and not (isinstance(g, int) and U + UNITS * g == 0):
                        take_rec(U, g)
                    if sl == SPLIT_AT and not last:
                        split_weights(hn + 1)
                return k

            split_weights(0)
            k = 0
            for it in PRE:
                aux(it, k, 0, 0, True, 0)
                k += 1
                if it == ("max", 0, QT - 1, KC - 1):
                    combine_max(0, 0, k)
            split_weights(1)
            for L in range(LEAD - 1):
                low_probs(L, 0)
            k = unit(0, 0, k, False)
            with dve.Fori(0, PAIRS - 1) as g:
                kk = k
                for U in range(1, UNITS + 1):
                    kk = unit(U, g, kk, False)
            for U in range(1, UNITS):
                k = unit(U, PAIRS - 1, k, True)
            take_rec(UNITS, PAIRS - 1)
            for it in (("turn_o", NQ - 1), ("out_proj", NQ - 1)):
                aux(it, k, PAIRS - 1, 0, False, 0)
                k += 1
            dve.wait_ge(ld_again, DMA)
            dve.wait_ge(aux_free, k + AP * (PAIRS - 1))
            for c in range(NQ):
                t = slice(QT * c, QT * c + QT)
                link(V.scalar_tensor_tensor(out=s_acc[:, t, :], in0=s_acc[:, t, :], scalar=wmax[:, 2:3],
                                            in1=bout_sb[:].unsqueeze(1).to_broadcast([P, QT, D]),
                                            op0=ALU.mult, op1=ALU.add))
                link(V.tensor_tensor(s_acc[:, t, :], s_acc[:, t, :], gate[:, t, :], ALU.mult))
                V.tensor_tensor(o_sb[:, t, :], s_acc[:, t, :], x_again[:, t, :], ALU.add).then_inc(fin, 1)

        @block.gpsimd
        def _(pool):
            G = nc.gpsimd
            pool.wait_ge(wmax_ready, 1)
            G.partition_all_reduce(wmax[:, 1:2], wmax[:, 0:1], P, RMAX).then_inc(wvall_ready, 1)
            pool.wait_ge(wvall_ready, 1)
            pool.wait_ge(gate_done, 4)
            for a in range(2):
                G.memset(km2[a][DH:DH + 2, :].bitcast(F32), 1.0).then_inc(const_ready, 1)
                pool.wait_ge(const_ready, 2 * a + 1)
                G.memset(v_sb[a][:, :, DH:DH + 1], 1.0).then_inc(const_ready, 1)
                pool.wait_ge(const_ready, 2 * a + 2)

            def rope_add(c, hn, k):
                pool.wait_ge(aux_free, k)
                G.tensor_tensor(turn2[:, c % 2, :], turn2[:, c % 2, :], fenc[:, c * 512:(c + 1) * 512], ALU.add).then_inc(rope_a, 1)
                pool.wait_ge(rope_a, 4 * hn + c + 1)
                G.tensor_tensor(turn1[:, c % 2, :], turn1[:, c % 2, :], turn2[:, c % 2, :], ALU.add).then_inc(rope_sum, 1)

            def low_part(c, hn):
                pool.wait_ge(hi_done, 4 * hn + c + 1)
                G.tensor_tensor(qk_lo[:, c * 512:(c + 1) * 512], turn1[:, c % 2, :],
                                qk_hi[:, c * 512:(c + 1) * 512].bitcast(F32), ALU.subtract).then_inc(lo_done, 1)

            def low_probs(L, g):
                pool.wait_ge(probs_ready, L + 1 + PAIR_STEPS * g)
                c = slice(dve_low(L), 2 * QC)
                G.tensor_tensor(pl[:, L % 4, c], pf[:, L % PF, c], ph[:, L % 4, c], ALU.subtract).then_inc(pl_pool, 1)

            def add_parts(U, g):
                pool.wait_ge(acc_copied, U + UNITS * g)
                r = o_raw[:, (U - 1) % 2, :, :]
                G.tensor_tensor(o_sum[:], r[:, :, 0:DH], r[:, :, DH + 1:OW], ALU.add).then_inc(osum_ready, 1)

            def normalise(U, g):
                pool.wait_ge(rec_ready, U + UNITS * g)
                pool.wait_ge(osum_ready, U + UNITS * g)
                qc, a = (U - 1) % NQ, ((U - 1) // NQ) % 2
                G.tensor_tensor(o_sb[:, QT * qc:QT * qc + QT, a * DH:(a + 1) * DH], o_sum[:],
                                o_rec[:, (U - 1) % 2, :].unsqueeze(2).to_broadcast([P, QT, DH]), ALU.mult).then_inc(o_ready, 1)

            def unit(U, g, k, last):
                hd = U // NQ
                hn = hd + 1 + 2 * g
                prep = not (last and hd % 2 == 1)
                rot_k = 0
                for s in range(STEPS):
                    L = U * STEPS + s
                    sl = STEPS * (U % NQ) + s
                    post = not (isinstance(g, int) and U + UNITS * g == 0)
                    if not (last and L + LEAD - 1 >= PAIR_STEPS):
                        low_probs(L + LEAD - 1, g)
                    for it in items(U, s, last):
                        k += 1
                        if it[0] == "rot":
                            rot_k = k + AP * g
                    if prep and sl - 1 in ROT_AT:
                        rope_add(ROT_AT.index(sl - 1), hn, rot_k)
                    if prep and sl - 3 in ROT_AT:
                        low_part(ROT_AT.index(sl - 3), hn)
                    if s == 1 and post:
                        add_parts(U, g)
                    if s == 2 and post:
                        normalise(U, g)
                return k

            k = 0
            for it in PRE:
                k += 1
                if it[0] == "rot":
                    rope_add(it[1], 0, k)
                    low_part(it[1], 0)
            for L in range(LEAD - 1):
                low_probs(L, 0)
            k = unit(0, 0, k, False)
            with pool.Fori(0, PAIRS - 1) as g:
                kk = k
                for U in range(1, UNITS + 1):
                    kk = unit(U, g, kk, False)
            for U in range(1, UNITS):
                k = unit(U, PAIRS - 1, k, True)
            add_parts(UNITS, PAIRS - 1)
            normalise(UNITS, PAIRS - 1)


def constants():
    freqs = (10000.0 ** (-np.arange(0, DH, 2, dtype=np.float64) / DH)).astype(np.float32)
    pos = np.arange(N, dtype=np.float32)[:, None]
    ang = (pos * freqs).astype(np.float64)
    cos = np.repeat(np.cos(ang), 2, axis=1).T.astype(np.float32)
    sin = np.repeat(np.sin(ang), 2, axis=1).T.astype(np.float32)
    sin[:DH // 2] *= -1
    ff = (pos * np.arange(1, 17, dtype=np.float32)).astype(np.float64)
    four = np.concatenate([np.sin(ff), np.cos(ff)], axis=1).T.astype(np.float32)
    expand = np.zeros((P, NBR, P), np.float32)
    for j in range(NBR):
        for c in range(P):
            expand[4 * j + c // 32, j, c] = expand[E + 4 * j + c // 32, j, c] = 1
    return {"cos": np.concatenate([cos, cos]), "sin": np.concatenate([sin, sin]), "four": four,
            "expand": expand, "eye": np.eye(P, dtype=np.float32)}


def kernel(**inputs):
    import numpy as _np
    import concourse.bacc as _bacc
    from concourse import mybir as _mybir
    from concourse.bass_utils import run_bass_kernel_spmd as _run

    i = {k.removeprefix("L0_"): _np.asarray(v) for k, v in inputs.items()}
    swap = _np.concatenate([_np.arange(1, DH, 2), _np.arange(0, DH, 2)])
    w = i["attn_w_qkv"].reshape(3, H, DH, D)
    w_head = _np.concatenate([w[0], w[1], w[0][:, swap], w[1][:, swap], w[2]], axis=1).transpose(0, 2, 1)
    w1 = _np.concatenate([i["ffn_w1"].transpose(1, 0, 2).reshape(D, -1), i["ffn_sw1"].transpose(1, 0, 2).reshape(D, -1)], axis=1)
    b1 = _np.concatenate([i["ffn_b1"].reshape(-1), i["ffn_sb1"].reshape(-1)]).reshape(NB, P).T
    w2 = _np.concatenate([i["ffn_w2"].reshape(-1, D), i["ffn_sw2"].reshape(-1, D)]).reshape(NB, P, D).transpose(1, 0, 2)
    wf = i["attn_w_fproj"].T
    bf = i["attn_b_fproj"][:, None]
    c = constants()
    arrays = {
        "x": i["attn_x"], "w_head": w_head, "wqkv_all": i["attn_w_qkv"].reshape(P, -1),
        "wf": _np.concatenate([wf, wf], axis=1), "bf": _np.concatenate([bf, bf]), "four": c["four"],
        "cos": c["cos"], "sin": c["sin"], "w_out": i["attn_w_out"].T.reshape(PAIRS, P, D),
        "b_out": _np.tile(i["attn_b_out"], (P, 1)), "rw": i["ffn_router_w"],
        "rb": _np.tile(i["ffn_router_b"], (P, 1)), "w1": w1, "b1": b1, "w2": w2,
        "b2": _np.concatenate([i["ffn_b2"], i["ffn_b2"]]), "sb2": i["ffn_sb2"].T, "expand": c["expand"], "eye": c["eye"],
    }
    arrays = {k: _np.ascontiguousarray(v) for k, v in arrays.items()}
    nc = _bacc.Bacc("TRN2", target_bir_lowering=False, num_devices=1)
    args = [nc.dram_tensor(k, v.shape, _mybir.dt.from_np(v.dtype), kind="ExternalInput").ap() for k, v in arrays.items()]
    args.append(nc.dram_tensor("out", (1, N, D), _mybir.dt.float32, kind="ExternalOutput").ap())
    program(nc, *args)
    r = _run(nc, [arrays], core_ids=[0])
    return r.results[0]["out"]
```

```python
from contextlib import ExitStack

import numpy as np

import concourse.bass as bass
from concourse import mybir

F32 = mybir.dt.float32
F32R = mybir.dt.float32r
F16 = mybir.dt.float16
U32 = mybir.dt.uint32
ALU = mybir.AluOpType
ACT = mybir.ActivationFunctionType
AX = mybir.AxisListType
RMAX = bass.bass_isa.ReduceOp.absmax

P = 128
N = 2048
D = 128
NT = N // P
H = 16
DH = 64
PAIRS = H // 2
QC = 512
NQ = N // QC
QT = QC // P
STEPS = N // (2 * P)
UNITS = 2 * NQ
PAIR_STEPS = UNITS * STEPS
PF = 4
KC = N // 512
LEAD = 3
WCOLS = 5 * DH
E = 64
TOPK = 8
HID = 2560
NB = HID // P
NBR = 2048 // P
NBS = NB - NBR
SHARED = NQ * NBS
DOWN = 3
EPS = 1e-5
SCALE = DH ** -0.5
VW = 2 * DH + 2
OW = 2 * DH + 1
DMA = 16
MOVES_MAX = 12
MOVES_REST = 6
MAX_AT = 2
PROJ_AT = (0, 3, 7, 9)
ROT_AT = (1, 5, 8, 11)
V_AT = (15, 17, 21, 23)
NV = len(V_AT)
VT = NT // NV
SPLIT_AT = 27


def dve_low(L):
    step = (L - LEAD + 1) % (NQ * STEPS)
    low = 640 if 11 <= step < 15 else 512 if step < 15 else 384
    if step == MAX_AT or step in (18, 26) or step in V_AT:
        low -= P
    return low


def items(U, s, last):
    out = []
    qc, a = U % NQ, (U // NQ) % 2
    sl = STEPS * qc + s
    M, m = (U + 2, s - MAX_AT) if s >= MAX_AT else (U + 1, s - MAX_AT + STEPS)
    if not (last and M >= UNITS):
        out += [("max", M, i // KC, i % KC) for i in (2 * m, 2 * m + 1)]
    if s == MAX_AT and not (last and U + 1 >= UNITS):
        out.append(("turn_max", U + 1))
    if not (last and a == 1):
        for kind, steps in (("proj", PROJ_AT), ("rot", ROT_AT), ("v", V_AT)):
            if sl in steps:
                out.append((kind, steps.index(sl)))
    if U > NQ and s == 4:
        out.append(("turn_o", (U - 1) % NQ))
    if U > NQ and s == 6:
        out.append(("out_proj", (U - 1) % NQ))
    return out


THIRD = {"v": 2, "turn_max": 5, "proj": 3, "rot": 4, "turn_o": 3, "out_proj": 4}


def head_items():
    return [(k, c) for c in range(4) for k in ("proj", "rot")] + [("v", i) for i in range(len(V_AT))]


def max_items(U):
    return [("max", U, i // KC, i % KC) for i in range(QT * KC)]


PRE = head_items() + max_items(0) + [("turn_max", 0)] + max_items(1)[:2 * (STEPS - MAX_AT)]
FIRST = PRE.index(("turn_max", 0)) + 4
AP = sum(len(items(U, s, False)) for U in range(1, UNITS + 1) for s in range(STEPS))


def program(nc, x, w_head, wqkv_all, wf, bf, four, cos, sin, w_out, b_out, rw, rb, w1, b1, w2, b2, sb2,
            expand, eye, out):
    ctx = ExitStack()
    with ctx:
        def sb(name, shape, dt, where=ctx):
            return where.enter_context(nc.sbuf_tensor(name, shape, dt))

        def sem(name):
            return ctx.enter_context(nc.semaphore(name))

        gate = sb("gate", [P, NT, D], F32)
        xh16 = sb("xh16", [P, N], F16)
        xl16 = sb("xl16", [P, N], F16)
        cos_sb = sb("cos_sb", [P, N], F32)
        sin_sb = sb("sin_sb", [P, N], F32)
        fenc = sb("fenc", [P, N], F32)
        eye_sb = sb("eye_sb", [P, P], F32)
        bout_sb = sb("bout_sb", [P, D], F32)
        wmax = sb("wmax", [P, 4], F32)
        early = ExitStack()
        with ExitStack() as over:
            four_sb = sb("four_sb", [32, N], F32, over)
        cwt = sb("cwt", [P, NT, 2, E], F32, early)
        logit = sb("logit", [P, NT, E], F32, early)
        prob = sb("prob", [P, NT, E], F32, early)
        rest = sb("rest", [P, NT, E], F32, early)
        with ExitStack() as over:
            xn = sb("xn", [P, NT, D], F32, over)
            w1_sb = sb("w1_sb", [P, HID], F32, over)
            w2_sb = sb("w2_sb", [P, HID], F32, over)
        wqkv_sb = sb("wqkv_sb", [P, 3 * H * DH], F32, early)
        hid_hi = sb("hid_hi", [P, 4, 512], F32R, early)
        hid_lo = sb("hid_lo", [P, 4, 512], F32R, early)
        x_hi = sb("x_hi", [P, N], F32R, early)
        x_lo = sb("x_lo", [P, N], F32R, early)
        stats = sb("stats", [P, NT, 6], F32, early)
        mv = sb("mv", [P, NT, 2], F32, early)
        rs = sb("rs", [P, 4, NT], F32, early)
        wf_sb = sb("wf_sb", [32, P], F32, early)
        bf_sb = sb("bf_sb", [P, 1], F32, early)
        rw_sb = sb("rw_sb", [P, E], F32, early)
        rw_hi = sb("rw_hi", [P, E], F32R, early)
        rw_lo = sb("rw_lo", [P, E], F32R, early)
        rb_sb = sb("rb_sb", [P, E], F32, early)
        top = sb("top", [P, NT, TOPK], F32, early)
        rstat = sb("rstat", [P, 5, NT], F32, early)
        cw = sb("cw", [P, N], F32R, early)
        ex = sb("ex", [P, NBR, P], F32R, early)
        w1_hi = sb("w1_hi", [P, HID], F32R, early)
        w1_lo = sb("w1_lo", [P, HID], F32R, early)
        b1_sb = sb("b1_sb", [P, NB], F32, early)
        w2_hi = sb("w2_hi", [P, HID], F32R, early)
        w2_lo = sb("w2_lo", [P, HID], F32R, early)
        b2_sb = sb("b2_sb", [P, D], F32, early)
        b2_hi = sb("b2_hi", [P, D], F32R, early)
        b2_lo = sb("b2_lo", [P, D], F32R, early)
        sb2_sb = sb("sb2_sb", [P, 2], F32, early)
        sb2_sum = sb("sb2_sum", [P, 1], F32, early)
        with ExitStack() as over:
            ex_in = sb("ex_in", [P, NBR, P], F32, over)
        hid = sb("hid", [P, 4, 512], F32, early)
        gate_t = sb("gate_t", [P, 512], F32, early)
        early.close()
        turn1 = sb("turn1", [P, 2, 512], F32)
        turn2 = sb("turn2", [P, 2, 512], F32)
        qk_hi = sb("qk_hi", [P, N], F32R)
        qk_lo = sb("qk_lo", [P, N], F32R)
        w_in = sb("w_in", [P, WCOLS], F32)
        w_hi = sb("w_hi", [P, WCOLS], F16)
        w_lo = sb("w_lo", [P, WCOLS], F16)
        qm1 = [sb(f"qm1_{a}", [P, N], F32R) for a in range(2)]
        km1 = [sb(f"km1_{a}", [P, N], F32R) for a in range(2)]
        qm2 = [sb(f"qm2_{a}", [P, N], F32R) for a in range(2)]
        km2 = [sb(f"km2_{a}", [P, N], F32R) for a in range(2)]
        v_sb = [sb(f"v_{a}", [P, NT, VW], F16) for a in range(2)]
        wo_sb = sb("wo_sb", [P, D], F32)
        pf = sb("pf", [P, PF, 2 * QC], F32)
        ph = sb("ph", [P, 4, 2 * QC], F16)
        pl = sb("pl", [P, 4, 2 * QC], F16)
        max_p = sb("max_p", [P, 2, QT, KC], F32)
        max_n = sb("max_n", [P, 2, QT], F32)
        max_r = sb("max_r", [QT, 2, 2, P], F32R)
        o_raw = sb("o_raw", [P, 2, QT, OW], F32)
        o_sum = sb("o_sum", [P, QT, DH], F32)
        o_rec = sb("o_rec", [P, 2, QT], F32)
        o_sb = sb("o_sb", [P, NT, 2 * DH], F32)
        ot_sb = sb("ot_sb", [P, QC], F32)
        s_acc = sb("s_acc", [P, NT, D], F32)

        ps_s = ctx.enter_context(nc.psum_tensor("ps_s", [P, 2, 2, 512], F32))
        with ExitStack() as over:
            ps_y = over.enter_context(nc.psum_tensor("ps_y", [P, N], F32))
        ps_a = ctx.enter_context(nc.psum_tensor("ps_a", [P, 2, 512], F32))
        ps_o = ctx.enter_context(nc.psum_tensor("ps_o", [P, 2, 512], F32))

        ld_again = sem("ld_again")
        ld_x = [sem(f"ld_x{c}") for c in range(4)]
        ld_four = sem("ld_four")
        ld_eye, ld_small, ld_w1, ld_w2, ld_ex = sem("ld_eye"), sem("ld_small"), sem("ld_w1"), sem("ld_w2"), sem("ld_ex")
        ld_pos, ld_wqkv = sem("ld_pos"), sem("ld_wqkv")
        dve_seq = sem("dve_seq")
        var_ready, std_ready = sem("var_ready"), sem("std_ready")
        xn_ready, xt_ready = sem("xn_ready"), sem("xt_ready")
        x_high, x_split = sem("x_high"), sem("x_split")
        rw_high, rw_split, b2_high, b2_split = sem("rw_high"), sem("rw_split"), sem("b2_high"), sem("b2_split")
        mlp_high, w1_split, w2_split = sem("mlp_high"), sem("w1_split"), sem("w2_split")
        ex_ready = sem("ex_ready")
        fenc_ready, fenc_done = sem("fenc_ready"), sem("fenc_done")
        wmax_ready, wvall_ready = sem("wmax_ready"), sem("wvall_ready")
        logit_ready, shifted, exps = sem("logit_ready"), sem("shifted"), sem("exps")
        cw_tok, cw_turned, cw_high, cw_ready = sem("cw_tok"), sem("cw_turned"), sem("cw_high"), sem("cw_ready")
        h_ready, c_ready, sil_ready = sem("h_ready"), sem("c_ready"), sem("sil_ready")
        hid_ready, y_done = sem("hid_ready"), sem("y_done")
        high_shared, high_routed, low_ready = sem("high_shared"), sem("high_routed"), sem("low_ready")
        gate_sil, gate_turned, gate_done = sem("gate_sil"), sem("gate_turned"), sem("gate_done")
        w_loaded, w_high, w_split = sem("w_loaded"), sem("w_high"), sem("w_split")
        wo_loaded = sem("wo_loaded")
        aux_ready, aux_free = sem("aux_ready"), sem("aux_free")
        v_high = sem("v_high")
        rope_a, rope_sum, hi_done, lo_done = sem("rope_a"), sem("rope_sum"), sem("hi_done"), sem("lo_done")
        moved_max, moved_rest = sem("moved_max"), sem("moved_rest")
        max_ready, max_high, max_rows = sem("max_ready"), sem("max_high"), sem("max_rows")
        s_ready, probs_ready = sem("s_ready"), sem("probs_ready")
        pl_dve, pl_pool = sem("pl_dve"), sem("pl_pool")
        pv_done, acc_copied = sem("pv_done"), sem("acc_copied")
        rec_ready, osum_ready, o_ready = sem("rec_ready"), sem("osum_ready"), sem("o_ready")
        const_ready, fin, stored = sem("const_ready"), sem("fin"), sem("stored")

        SMALL = 5
        x_again = qk_hi[:].bitcast(F32).rearrange("p (t d) -> p t d", d=D)
        out_v = out[0].rearrange("(t p) d -> p t d", p=P)

        def aux_bank(k):
            four = len(head_items()) <= k < len(PRE) and k % 4 >= 2
            return (ps_o if four else ps_a)[:, k % 2, :]

        block = ctx.enter_context(nc.Block())

        @block.sync
        def _(sp):
            for dst, src in ((wf_sb, wf), (bf_sb, bf), (four_sb, four)):
                sp.dma_start(dst[:], src).then_inc(ld_four, DMA)
            x_v = x[0].rearrange("(t p) d -> p t d", p=P)
            for c in range(4):
                sp.dma_start(gate[:, 4 * c:4 * c + 4, :], x_v[:, 4 * c:4 * c + 4, :]).then_inc(ld_x[c], DMA)
            sp.dma_start(eye_sb[:], eye).then_inc(ld_eye, DMA)
            for dst, src in ((rw_sb, rw), (rb_sb, rb), (b1_sb, b1), (b2_sb, b2), (sb2_sb, sb2)):
                sp.dma_start(dst[:], src).then_inc(ld_small, DMA)
            sp.dma_start(w1_sb[:], w1).then_inc(ld_w1, DMA)
            sp.dma_start(w2_sb[:], w2).then_inc(ld_w2, DMA)
            sp.dma_start(ex_in[:], expand).then_inc(ld_ex, DMA)
            for dst, src in ((cos_sb, cos), (sin_sb, sin), (bout_sb, b_out)):
                sp.dma_start(dst[:], src).then_inc(ld_pos, DMA)
            sp.wait_ge(w1_split, 1)
            sp.dma_start(wqkv_sb[:], wqkv_all).then_inc(ld_wqkv, DMA)
            sp.wait_ge(wmax_ready, 1)
            sp.wait_ge(cw_turned, 4)
            sp.dma_start(w_in[:], w_head[0]).then_inc(w_loaded, DMA)
            sp.wait_ge(gate_done, 4)

            def move(first, end, a, chunks):
                sp.wait_ge(lo_done, chunks + end)
                c = slice(first * 512, end * 512)
                for dst, src, p0 in ((qm1[a][0:DH, c], qk_hi, 0), (qm1[a][DH:P, c], qk_lo, 0),
                                     (km1[a][0:DH, c], qk_hi, DH), (km1[a][DH:P, c], qk_hi, DH)):
                    sp.dma_start(dst.bitcast(F32), src[p0:p0 + DH, c].bitcast(F32)).then_inc(moved_max, DMA)
                for dst, src, p0 in ((qm2[a][0:DH, c], qk_hi, 0), (km2[a][0:DH, c], qk_lo, DH)):
                    sp.dma_start(dst.bitcast(F32), src[p0:p0 + DH, c].bitcast(F32)).then_inc(moved_rest, DMA)

            def max_row(U, consumed):
                a, qc = (U // NQ) % 2, U % NQ
                sp.wait_ge(aux_free, consumed)
                for part in range(2):
                    sp.dma_start(qm2[a][DH + part:DH + part + 1, qc * QC:(qc + 1) * QC].bitcast(F32)
                                 .rearrange("o (t q) -> o t q", t=QT),
                                 max_r[:, U % 2, part, :].bitcast(F32)).then_inc(max_rows, DMA)

            def unit(U, g, k, last):
                qc, hd = U % NQ, U // NQ
                a = hd % 2
                if U == 1:
                    sp.wait_ge(aux_ready, k + AP * g)
                    sp.dma_start(wo_sb[:], w_out[g]).then_inc(wo_loaded, DMA)
                for s in range(STEPS):
                    for it in items(U, s, last):
                        k += 1
                        if it[0] == "turn_max":
                            max_row(it[1], k + AP * g)
                    if qc == 1 and s == MAX_AT and not (last and a == 1):
                        for first, end in ((0, 2), (2, 3), (3, 4)):
                            move(first, end, 1 - a, 4 * (hd + 1) + 8 * g)
                if qc == 1 and not last:
                    sp.wait_ge(w_split, hd + 2 + 2 * g)
                    sp.dma_start(w_in[:], w_head[g * 2 + (hd + 2)]).then_inc(w_loaded, DMA)
                return k

            sp.wait_ge(lo_done, 4)
            for dst, src, p0 in ((qm1[0][0:DH, :], qk_hi, 0), (qm1[0][DH:P, :], qk_lo, 0),
                                 (km1[0][0:DH, :], qk_hi, DH), (km1[0][DH:P, :], qk_hi, DH)):
                sp.dma_start(dst.bitcast(F32), src[p0:p0 + DH, :].bitcast(F32)).then_inc(moved_max, DMA)
            for dst, src, p0 in ((qm2[0][0:DH, :], qk_hi, 0), (km2[0][0:DH, :], qk_lo, DH)):
                sp.dma_start(dst.bitcast(F32), src[p0:p0 + DH, :].bitcast(F32)).then_inc(moved_rest, DMA)
            sp.wait_ge(w_split, 1)
            sp.dma_start(w_in[:], w_head[1]).then_inc(w_loaded, DMA)
            k = 0
            for it in PRE:
                k += 1
                if it[0] == "turn_max":
                    max_row(0, k)
            k = unit(0, 0, k, False)
            with sp.Fori(0, PAIRS - 1) as g:
                kk = k
                for U in range(1, UNITS + 1):
                    kk = unit(U, g, kk, False)
            for U in range(1, UNITS):
                if U == NQ:
                    sp.wait_ge(moved_max, DMA * (4 + MOVES_MAX * (H - 1)))
                    sp.wait_ge(moved_rest, DMA * (2 + MOVES_REST * (H - 1)))
                    sp.dma_start(x_again, x[0].rearrange("(t p) d -> p t d", p=P)).then_inc(ld_again, DMA)
                k = unit(U, PAIRS - 1, k, True)
            for c in range(NQ):
                sp.wait_ge(fin, c + 1)
                sp.dma_start(out_v[:, QT * c:QT * c + QT, :], o_sb[:, QT * c:QT * c + QT, :]).then_inc(stored, DMA)
            sp.wait_ge(stored, NQ * DMA)

        @block.tensor
        def _(pe):
            mm = nc.tensor.matmul

            def mm3(dst, s_hi, s_lo, m_hi, m_lo, start=True, stop=True):
                mm(dst, s_hi, m_hi, start=start, stop=False)
                mm(dst, s_lo, m_hi, start=False, stop=False)
                return mm(dst, s_hi, m_lo, start=False, stop=stop)

            def aux(it, k, g, hn, wo_count, turned):
                kind = it[0]
                dst = aux_bank(k)
                if k >= 2:
                    pe.wait_ge(aux_free, k - 3 if len(head_items()) + 4 <= k < len(PRE) else k - 1 + AP * g)
                if kind == "max":
                    _, U, qt, kc = it
                    a, qc = (U // NQ) % 2, U % NQ
                    if qc == 0 and qt == 0 and kc == 0:
                        pe.wait_ge(moved_max, DMA * (4 + MOVES_MAX * (U // NQ)) + 2 * DMA * MOVES_MAX * g)
                    q0 = qc * QC + qt * P
                    last = mm(dst, qm1[a][:, q0:q0 + P], km1[a][:, kc * 512:(kc + 1) * 512], start=True, stop=True)
                elif kind == "turn_max":
                    U = it[1]
                    pe.wait_ge(max_ready, U + 1 + UNITS * g)
                    last = mm(dst[0:QT, 0:P], max_n[:, U % 2, :], eye_sb[:], start=True, stop=True)
                elif kind in ("proj", "rot"):
                    if it == ("proj", 0):
                        pe.wait_ge(w_split, hn + 1)
                    w = slice(0, P) if kind == "proj" else slice(P, 2 * P)
                    t = slice(it[1] * 512, (it[1] + 1) * 512)
                    last = mm3(dst, w_hi[:, w], w_lo[:, w], xh16[:, t], xl16[:, t])
                elif kind == "v":
                    for i in range(VT):
                        t = slice((VT * it[1] + i) * P, (VT * it[1] + i + 1) * P)
                        last = mm3(dst[:, i * DH:(i + 1) * DH], xh16[:, t], xl16[:, t], w_hi[:, 2 * P:], w_lo[:, 2 * P:])
                elif kind == "turn_o":
                    pe.wait_ge(o_ready, NQ + it[1] + 1 + UNITS * g)
                    for i in range(QT):
                        last = nc.tensor.transpose(dst[:, i * P:(i + 1) * P], o_sb[:, QT * it[1] + i, :], eye_sb[:])
                else:
                    pe.wait_ge(aux_free, turned + AP * g)
                    pe.wait_ge(wo_loaded, wo_count)
                    for i in range(QT):
                        last = mm(dst[:, i * P:(i + 1) * P], ot_sb[:, i * P:(i + 1) * P], wo_sb[:], start=True, stop=True)
                last.then_inc(aux_ready, 1)

            pe.wait_ge(ld_four, 3 * DMA)
            for c in range(4):
                mm(ps_s[:, c // 2, c % 2, :], wf_sb[:], four_sb[:, c * 512:(c + 1) * 512], start=True, stop=True)\
                    .then_inc(fenc_ready, 1)
            pe.wait_ge(ld_eye, DMA)
            for c in range(4):
                pe.wait_ge(xn_ready, c + 1)
                for i in range(4):
                    last = nc.tensor.transpose(ps_y[:, c * 512 + i * P:c * 512 + (i + 1) * P], xn[:, 4 * c + i, :], eye_sb[:])
                last.then_inc(xt_ready, 1)
            pe.wait_ge(rw_split, 1)
            pe.wait_ge(fenc_done, 4)
            for i in range(NT):
                if i % 4 == 0:
                    pe.wait_ge(x_split, i // 4 + 1)
                dst = ps_s[:, i // 8, 1, (i % 8) * E:(i % 8 + 1) * E]
                t = slice(i * P, (i + 1) * P)
                mm3(dst, x_hi[:, t], x_lo[:, t], rw_hi[:], rw_lo[:], stop=False)
                last = mm(dst, x_lo[:, t], rw_lo[:], start=False, stop=True)
            last.then_inc(logit_ready, 1)

            def up(tc, j, n):
                if not (isinstance(n, int) and n < 2):
                    pe.wait_ge(sil_ready, n - 1)
                c = slice(j * P, (j + 1) * P)
                tok = bass.ts(tc, 512)
                mm3(ps_s[:, j % 2, 0, :], w1_hi[:, c], w1_lo[:, c], x_hi[:, tok], x_lo[:, tok]).then_inc(h_ready, 1)
                if j < NBR:
                    if not (isinstance(n, int) and n < SHARED + 2):
                        pe.wait_ge(hid_ready, n - (SHARED + 1))
                    mm(ps_s[:, j % 2, 1, :], ex[:, j, :], cw[:, tok], start=True, stop=True).then_inc(c_ready, 1)

            def down(tc, j, n):
                pe.wait_ge(low_ready, n + 1)
                c = slice(j * P, (j + 1) * P)
                mm3(ps_y[:, bass.ts(tc, 512)], w2_hi[:, c], w2_lo[:, c], hid_hi[:, j % 4, :], hid_lo[:, j % 4, :],
                    start=(j == NBR), stop=(j == NBR - 1)).then_inc(y_done, 1)

            def down_b2(tc):
                mm(ps_y[:, bass.ts(tc, 512)], b2_hi[:], cw[:, bass.ts(tc, 512)], start=False, stop=False)
                mm(ps_y[:, bass.ts(tc, 512)], b2_lo[:], cw[:, bass.ts(tc, 512)], start=False, stop=False)

            def turn_gate(tc):
                pe.wait_ge(gate_sil, tc + 1)
                for i in range(4):
                    last = mm(ps_y[:, bass.ds(tc * 512 + i * P, P)], gate_t[:, i * P:(i + 1) * P], eye_sb[:], start=True, stop=True)
                last.then_inc(gate_turned, 1)

            pe.wait_ge(w1_split, 1)
            for i in range(NBS):
                up(0, NBR + i, i)
                if i >= DOWN:
                    down(0, NBR + i - DOWN, i - DOWN)
            def shared_chunk(t):
                for i in range(NBS):
                    up(t + 1, NBR + i, t * NBS + (NBS + i))
                    if i < DOWN:
                        down(t, NB - DOWN + i, t * NBS + (NBS + i - DOWN))
                    else:
                        down(t + 1, NBR + i - DOWN, t * NBS + (NBS + i - DOWN))
                    if isinstance(t, int):
                        turn_weights(i)

            def turn_weights(c):
                pe.wait_ge(cw_tok, 1)
                if c >= 2:
                    pe.wait_ge(cw_ready, c - 1)
                for i in range(4):
                    last = nc.tensor.transpose(ps_s[:, c % 2, 1, i * P:(i + 1) * P], cwt[:, 4 * c + i, :, :], eye_sb[:])
                last.then_inc(cw_turned, 1)

            with pe.Fori(0, NQ - 2) as t:
                shared_chunk(t)
            shared_chunk(NQ - 2)
            pe.wait_ge(cw_ready, 4)
            pe.wait_ge(ex_ready, 1)
            pe.wait_ge(b2_split, 1)
            for j in range(NBR):
                up(0, j, SHARED + j)
                if j < DOWN:
                    down(NQ - 1, NB - DOWN + j, SHARED - DOWN + j)
                else:
                    if j == DOWN:
                        down_b2(0)
                    down(0, j - DOWN, SHARED + j - DOWN)
            def routed_chunk(t):
                for j in range(NBR):
                    up(t + 1, j, t * NBR + (SHARED + NBR + j))
                    if j < DOWN:
                        down(t, NBR - DOWN + j, t * NBR + (SHARED + NBR + j - DOWN))
                    else:
                        if j == DOWN:
                            down_b2(t + 1)
                        down(t + 1, j - DOWN, t * NBR + (SHARED + NBR + j - DOWN))
                    if j == 6:
                        turn_gate(t)
                    if isinstance(t, int) and j % 2 == 1:
                        if j == 1:
                            pe.wait_ge(gate_done, 2)
                        aux(PRE[j // 2], j // 2, 0, 0, 0, 0)

            with pe.Fori(0, NQ - 2) as t:
                routed_chunk(t)
            routed_chunk(NQ - 2)
            for j in range(NBR - DOWN, NBR):
                down(NQ - 1, j, SHARED + (NQ - 1) * NBR + j)
            turn_gate(NQ - 1)

            pe.wait_ge(gate_done, 4)

            def scores(L, i, g):
                U = L // STEPS
                a, qc = (U // NQ) % 2, U % NQ
                if L % STEPS == 0 and i == 0:
                    if qc == 0:
                        pe.wait_ge(moved_rest, DMA * (2 + MOVES_REST * (U // NQ)) + 2 * DMA * MOVES_REST * g)
                    pe.wait_ge(max_rows, 2 * DMA * (U + 1) + 2 * DMA * UNITS * g)
                if L >= 2 and i == 0:
                    pe.wait_ge(probs_ready, L - 1 + PAIR_STEPS * g)
                q = slice(qc * QC, (qc + 1) * QC)
                kt = slice((2 * (L % STEPS) + i) * P, (2 * (L % STEPS) + i + 1) * P)
                mm(ps_s[:, L % 2, i, :], km1[a][:, kt], qm1[a][:, q], start=True, stop=False)
                last = mm(ps_s[:, L % 2, i, :], km2[a][0:DH + 2, kt], qm2[a][0:DH + 2, q], start=False, stop=True)
                if i == 1:
                    last.then_inc(s_ready, 1)

            def times_v(L, n, g):
                U = L // STEPS
                a = (U // NQ) % 2
                if n == 0:
                    if L % STEPS == 0 and not (isinstance(g, int) and U + UNITS * g == 0):
                        pe.wait_ge(acc_copied, U + UNITS * g)
                    if isinstance(g, int) and g == 0 and L == 0:
                        pe.wait_ge(aux_free, len(PRE))
                    pe.wait_ge(pl_dve, L + 1 + PAIR_STEPS * g)
                if n == dve_low(L) // P:
                    pe.wait_ge(pl_pool, L + 1 + PAIR_STEPS * g)
                i, qt = n // QT, n % QT
                kt = 2 * (L % STEPS) + i
                dst = ps_o[:, qt // 2, (qt % 2) * 256:(qt % 2) * 256 + OW]
                c = slice(i * QC + qt * P, i * QC + (qt + 1) * P)

                def high(start, stop):
                    return mm(dst, ph[:, L % 4, c], v_sb[a][:, kt, 0:OW], start=start, stop=stop, skip_group_check=True)

                def low(start, stop):
                    return mm(dst[:, 0:DH + 1], pl[:, L % 4, c], v_sb[a][:, kt, 0:DH + 1], start=start, stop=stop,
                              skip_group_check=True)

                if n < 2 * QT - 1:
                    high(kt == 0 and qt % 2 == 0, False)
                    low(False, kt == NT - 1)
                else:
                    low(False, False)
                    high(False, kt == NT - 1).then_inc(pv_done, 1)

            def unit(U, g, k, last):
                turned = 0
                for s in range(STEPS):
                    L = U * STEPS + s
                    work, n = items(U, s, last), 0
                    parts = [(times_v, L, i) for i in range(2 * QT)]
                    if not (last and L + LEAD >= PAIR_STEPS):
                        parts = [(scores, L + LEAD, i) for i in range(2)] + parts
                    for what, step, i in parts:
                        what(step, i, g)
                        if n < len(work) and (what is scores or (what is times_v and i >= (THIRD[work[n][0]] if n == 2 else 6))):
                            aux(work[n], k, g, U // NQ + 1 + 2 * g, DMA * (g + 1), turned)
                            k, n = k + 1, n + 1
                            if work[n - 1][0] == "turn_o":
                                turned = k
                    assert n == len(work)
                return k

            for k in range(8, len(PRE)):
                aux(PRE[k], k, 0, 0, 0, 0)
                if k == FIRST:
                    pe.wait_ge(const_ready, 4)
                if k in (FIRST, FIRST + 3, FIRST + 6):
                    scores((k - FIRST) // 3, 0, 0)
                    scores((k - FIRST) // 3, 1, 0)
            k = len(PRE)
            k = unit(0, 0, k, False)
            with pe.Fori(0, PAIRS - 1) as g:
                kk = k
                for U in range(1, UNITS + 1):
                    kk = unit(U, g, kk, False)
            for U in range(1, UNITS):
                k = unit(U, PAIRS - 1, k, True)
            for it in (("turn_o", NQ - 1), ("out_proj", NQ - 1)):
                aux(it, k, PAIRS - 1, 0, DMA * PAIRS, k)
                k += 1

        @block.scalar
        def _(act):
            act.wait_ge(var_ready, 1)
            nc.scalar.activation(rs[:, 1, :], rs[:, 0, :], ACT.Sqrt).then_inc(std_ready, 1)
            act.wait_ge(ld_four, 3 * DMA)
            for c in range(4):
                act.wait_ge(fenc_ready, c + 1)
                nc.scalar.activation(fenc[:, c * 512:(c + 1) * 512], ps_s[:, c // 2, c % 2, :], ACT.Identity,
                                     bias=bf_sb[:, 0:1]).then_inc(fenc_done, 1)
            for c in range(4):
                act.wait_ge(xt_ready, c + 1)
                t = slice(c * 512, (c + 1) * 512)
                nc.scalar.activation(x_hi[:, t], ps_y[:, t], ACT.Copy).then_inc(x_high, 1)
                nc.scalar.activation(xh16[:, t], ps_y[:, t], ACT.Copy).then_inc(x_high, 1)
            act.wait_ge(ld_w1, DMA)
            nc.scalar.activation(w1_hi[:], w1_sb[:], ACT.Copy).then_inc(mlp_high, 1)
            act.wait_ge(ld_w2, DMA)
            nc.scalar.activation(w2_hi[:], w2_sb[:], ACT.Copy).then_inc(mlp_high, 1)
            act.wait_ge(shifted, 1)
            nc.scalar.activation(prob[:], logit[:], ACT.Exp).then_inc(exps, 1)

            def high_part(c, hn, first):
                if c == 0 and not first:
                    act.wait_ge(moved_max, DMA * (4 + MOVES_MAX * (hn - 1)))
                    act.wait_ge(moved_rest, DMA * (2 + MOVES_REST * (hn - 1)))
                act.wait_ge(rope_sum, 4 * hn + c + 1)
                nc.scalar.activation(qk_hi[:, c * 512:(c + 1) * 512], turn1[:, c % 2, :], ACT.Copy).then_inc(hi_done, 1)

            def silu(j, n):
                act.wait_ge(h_ready, n + 1)
                if not (isinstance(n, int) and n < 4):
                    act.wait_ge(low_ready, n - 3)
                nc.scalar.activation(hid[:, j % 4, :], ps_s[:, j % 2, 0, :], ACT.Silu, bias=b1_sb[:, j:j + 1])\
                    .then_inc(sil_ready, 1)

            def high_hidden(j, n):
                act.wait_ge(sil_ready, n + 1)
                if not (isinstance(n, int) and n < 4):
                    act.wait_ge(y_done, n - 3)
                nc.scalar.activation(hid_hi[:, j % 4, :], hid[:, j % 4, :], ACT.Copy).then_inc(high_shared, 1)

            def silu_gate(tc):
                act.wait_ge(y_done, tc * NBR + (SHARED + NBR))
                if not (isinstance(tc, int) and tc == 0):
                    act.wait_ge(gate_turned, tc)
                nc.scalar.activation(gate_t[:], ps_y[:, bass.ts(tc, 512)], ACT.Silu, bias=sb2_sum[:, 0:1]).then_inc(gate_sil, 1)

            act.wait_ge(ex_ready, 1)
            act.wait_ge(ld_small, SMALL * DMA)
            act.wait_ge(w2_split, 1)
            for i in range(NBS):
                silu(NBR + i, i)
                high_hidden(NBR + i, i)
            with act.Fori(0, NQ - 1) as t:
                for i in range(NBS):
                    silu(NBR + i, t * NBS + (NBS + i))
                    high_hidden(NBR + i, t * NBS + (NBS + i))
            act.wait_ge(b2_split, 1)
            for j in range(NBR):
                silu(j, SHARED + j)
            def routed_chunk(t):
                for j in range(NBR):
                    silu(j, t * NBR + (SHARED + NBR + j))
                    if j == 4:
                        silu_gate(t)
                    if isinstance(t, int) and j in (5, 9, 13):
                        high_part(j // 4 - 1, 0, True)

            with act.Fori(0, NQ - 2) as t:
                routed_chunk(t)
            routed_chunk(NQ - 2)
            high_part(3, 0, True)
            silu_gate(NQ - 1)
            act.wait_ge(gate_done, 4)

            def exp_step(L, g, between=None):
                act.wait_ge(s_ready, L + 1 + PAIR_STEPS * g)
                if L >= PF:
                    act.wait_ge(pl_dve, L - PF + 1 + PAIR_STEPS * g)
                    act.wait_ge(pl_pool, L - PF + 1 + PAIR_STEPS * g)
                if L >= 4:
                    act.wait_ge(pv_done, L - 3 + PAIR_STEPS * g)
                nc.scalar.activation(pf[:, L % PF, :].rearrange("p (i q) -> p i q", i=2), ps_s[:, L % 2, :, :],
                                     ACT.Exp, scale=SCALE)
                if between:
                    between()
                nc.scalar.activation(ph[:, L % 4, :].rearrange("p (i q) -> p i q", i=2), ps_s[:, L % 2, :, :],
                                     ACT.Exp, scale=SCALE).then_inc(probs_ready, 1)

            def take_sums(U, g):
                act.wait_ge(pv_done, STEPS * U + PAIR_STEPS * g)
                nc.scalar.activation(o_raw[:, (U - 1) % 2, :, :].rearrange("p (b i) c -> p b i c", b=2),
                                     ps_o[:].rearrange("p b (i c) -> p b i c", i=2)[:, :, :, 0:OW],
                                     ACT.Copy).then_inc(acc_copied, 1)

            def unit(U, g, last):
                for s in range(STEPS):
                    L = U * STEPS + s
                    sums = (lambda: take_sums(U + 1, g)) if s == STEPS - 1 else None
                    if not (last and L + LEAD >= PAIR_STEPS):
                        exp_step(L + LEAD, g, sums)
                    elif sums:
                        sums()
                    sl = STEPS * (U % NQ) + s
                    if sl - 2 in ROT_AT and not (last and U // NQ == 1):
                        high_part(ROT_AT.index(sl - 2), U // NQ + 1 + 2 * g, False)

            for L in range(LEAD):
                exp_step(L, 0)
            unit(0, 0, False)
            with act.Fori(0, PAIRS - 1) as g:
                for U in range(1, UNITS + 1):
                    unit(U, g, False)
            for U in range(1, UNITS):
                unit(U, PAIRS - 1, True)

        @block.vector
        def _(dve):
            V = nc.vector
            seq = [0]

            def link(ins):
                seq[0] += 1
                ins.then_inc(dve_seq, 1)
                dve.wait_ge(dve_seq, seq[0])

            for i in range(NT):
                if i % 4 == 0:
                    dve.wait_ge(ld_x[i // 4], DMA)
                st = V.bn_stats(stats[:, i, :], gate[:, i, :])
            link(st)
            for i in range(NT):
                st = V.bn_aggr(mv[:, i, :], stats[:, i, :])
            link(st)
            V.tensor_scalar(rs[:, 0, :], mv[:, :, 1], EPS, None, ALU.add).then_inc(var_ready, 1)
            dve.wait_ge(std_ready, 1)
            link(V.reciprocal(rs[:, 2, :], rs[:, 1, :]))
            link(V.tensor_tensor(rs[:, 3, :], rs[:, 2, :], rs[:, 2, :], ALU.mult))
            link(V.tensor_tensor(rs[:, 1, :], rs[:, 3, :], rs[:, 0, :], ALU.mult))
            link(V.tensor_scalar(rs[:, 3, :], rs[:, 1, :], -0.5, 1.5, ALU.mult, ALU.add))
            link(V.tensor_tensor(rs[:, 1, :], rs[:, 3, :], rs[:, 2, :], ALU.mult))
            for i in range(NT):
                ins = V.tensor_scalar(xn[:, i, :], gate[:, i, :], mv[:, i, 0:1], rs[:, 1, i:i + 1], ALU.subtract, ALU.mult)
                if i % 4 == 3:
                    ins.then_inc(xn_ready, 1)
            dve.wait_ge(ld_small, SMALL * DMA)
            V.tensor_copy(rw_hi[:], rw_sb[:]).then_inc(rw_high, 1)
            V.tensor_copy(b2_hi[:], b2_sb[:]).then_inc(b2_high, 1)
            V.tensor_tensor(sb2_sum[:], sb2_sb[:, 0:1], sb2_sb[:, 1:2], ALU.add)
            dve.wait_ge(rw_high, 1)
            V.tensor_tensor(rw_lo[:], rw_sb[:], rw_hi[:].bitcast(F32), ALU.subtract).then_inc(rw_split, 1)
            dve.wait_ge(b2_high, 1)
            V.tensor_tensor(b2_lo[:], b2_sb[:], b2_hi[:].bitcast(F32), ALU.subtract).then_inc(b2_split, 1)
            for c in range(4):
                t = slice(c * 512, (c + 1) * 512)
                dve.wait_ge(x_high, 2 * c + 2)
                V.tensor_tensor(x_lo[:, t], ps_y[:, t], x_hi[:, t].bitcast(F32), ALU.subtract)
                V.tensor_tensor(xl16[:, t], ps_y[:, t], xh16[:, t], ALU.subtract).then_inc(x_split, 1)
            dve.wait_ge(mlp_high, 1)
            V.tensor_tensor(w1_lo[:], w1_sb[:], w1_hi[:].bitcast(F32), ALU.subtract).then_inc(w1_split, 1)
            dve.wait_ge(ld_ex, DMA)
            V.tensor_copy(ex[:], ex_in[:]).then_inc(ex_ready, 1)
            dve.wait_ge(logit_ready, 1)
            for b in range(2):
                ins = V.tensor_tensor(logit[:, 8 * b:8 * b + 8, :], ps_s[:, b, 1, :].rearrange("p (t e) -> p t e", t=8),
                                      rb_sb[:].unsqueeze(1).to_broadcast([P, 8, E]), ALU.add)
            link(ins)
            link(V.tensor_reduce(rstat[:, 0, :], logit[:], AX.X, ALU.max))
            V.tensor_tensor(logit[:], logit[:], rstat[:, 0, :].unsqueeze(2).to_broadcast([P, NT, E]), ALU.subtract)\
                .then_inc(shifted, 1)
            dve.wait_ge(ld_wqkv, DMA)
            V.tensor_reduce(wmax[:, 0:1], wqkv_sb[:], AX.X, ALU.max, apply_absolute_value=True).then_inc(wmax_ready, 1)
            dve.wait_ge(exps, 1)
            link(V.tensor_reduce(rstat[:, 1, :], prob[:], AX.X, ALU.add))
            link(V.reciprocal(rstat[:, 2, :], rstat[:, 1, :]))
            link(V.tensor_tensor(prob[:], prob[:], rstat[:, 2, :].unsqueeze(2).to_broadcast([P, NT, E]), ALU.mult))
            for i in range(NT):
                ins = V.max(top[:, i, :], prob[:, i, :])
            link(ins)
            for i in range(NT):
                ins = V.match_replace(rest[:, i, :], top[:, i, :], prob[:, i, :], 0.0)
            link(ins)
            V.tensor_tensor(logit[:], prob[:], rest[:], ALU.subtract)
            link(V.tensor_reduce(rstat[:, 3, :], top[:], AX.X, ALU.add))
            link(V.reciprocal(rstat[:, 4, :], rstat[:, 3, :]))
            dve.wait_ge(fenc_done, 4)
            for i in range(2):
                ins = V.tensor_tensor(cwt[:, :, i, :], logit[:], rstat[:, 4, :].unsqueeze(2).to_broadcast([P, NT, E]), ALU.mult)
            ins.then_inc(cw_tok, 1)
            for c in range(4):
                dve.wait_ge(cw_turned, c + 1)
                t = slice(c * 512, (c + 1) * 512)
                V.tensor_copy(cw[:, t], ps_s[:, c % 2, 1, :]).then_inc(cw_high, 1)
                dve.wait_ge(cw_high, c + 1)
                V.tensor_tensor(cw[E:, t], ps_s[E:, c % 2, 1, :], cw[E:, t].bitcast(F32), ALU.subtract).then_inc(cw_ready, 1)

            def split_weights(hn):
                dve.wait_ge(w_loaded, DMA * (hn + 1))
                V.tensor_scalar(w_hi[:], w_in[:], wmax[:, 3:4], None, ALU.mult).then_inc(w_high, 1)
                dve.wait_ge(w_high, hn + 1)
                V.scalar_tensor_tensor(out=w_lo[:], in0=w_in[:], scalar=wmax[:, 3:4], in1=w_hi[:],
                                       op0=ALU.mult, op1=ALU.subtract).then_inc(w_split, 1)

            def aux(it, k, g, hn, first, vpar):
                kind = it[0]
                src = aux_bank(k)
                dve.wait_ge(aux_ready, k + 1 + AP * g)
                if kind == "max":
                    _, U, qt, kc = it
                    V.tensor_reduce(max_p[:, U % 2, qt, kc:kc + 1], src, AX.X, ALU.max).then_inc(aux_free, 1)
                elif kind == "turn_max":
                    U = it[1]
                    if not (isinstance(g, int) and U + UNITS * g < 2):
                        dve.wait_ge(max_rows, 2 * DMA * (U - 1) + 2 * DMA * UNITS * g)
                    src = src[0:QT, 0:P]
                    V.tensor_copy(max_r[:, U % 2, 0, :], src).then_inc(max_high, 1)
                    dve.wait_ge(max_high, U + 1 + UNITS * g)
                    V.tensor_tensor(max_r[:, U % 2, 1, :], src, max_r[:, U % 2, 0, :].bitcast(F32), ALU.subtract)\
                        .then_inc(aux_free, 1)
                elif kind == "proj":
                    c = it[1]
                    if not (first and c < 2):
                        dve.wait_ge(lo_done, 4 * hn + (c - 1))
                    V.scalar_tensor_tensor(out=turn1[:, c % 2, :], in0=src, scalar=wmax[:, 2:3],
                                           in1=cos_sb[:, c * 512:(c + 1) * 512], op0=ALU.mult, op1=ALU.mult).then_inc(aux_free, 1)
                elif kind == "rot":
                    c = it[1]
                    V.scalar_tensor_tensor(out=turn2[:, c % 2, :], in0=src, scalar=wmax[:, 2:3],
                                           in1=sin_sb[:, c * 512:(c + 1) * 512], op0=ALU.mult, op1=ALU.mult).then_inc(aux_free, 1)
                elif kind == "v":
                    src = src[:, 0:VT * DH].rearrange("p (t d) -> p t d", t=VT)
                    t = slice(VT * it[1], VT * it[1] + VT)
                    V.tensor_copy(v_sb[vpar][:, t, 0:DH], src).then_inc(v_high, 1)
                    dve.wait_ge(v_high, NV * hn + (it[1] + 1))
                    V.tensor_tensor(v_sb[vpar][:, t, DH + 1:OW], src, v_sb[vpar][:, t, 0:DH], ALU.subtract).then_inc(aux_free, 1)
                elif kind == "turn_o":
                    V.tensor_copy(ot_sb[:], src).then_inc(aux_free, 1)
                else:
                    t = slice(QT * it[1], QT * it[1] + QT)
                    V.tensor_tensor(s_acc[:, t, :], src.rearrange("p (t d) -> p t d", t=QT), s_acc[:, t, :], ALU.add)\
                        .then_inc(aux_free, 1)

            def rope_add(c):
                dve.wait_ge(aux_free, 2 * c + 2)
                dve.wait_ge(fenc_done, 4)
                V.tensor_tensor(turn2[:, c % 2, :], turn2[:, c % 2, :], fenc[:, c * 512:(c + 1) * 512], ALU.add).then_inc(rope_a, 1)
                dve.wait_ge(rope_a, c + 1)
                V.tensor_tensor(turn1[:, c % 2, :], turn1[:, c % 2, :], turn2[:, c % 2, :], ALU.add).then_inc(rope_sum, 1)

            def weigh(j, n):
                m = n - SHARED
                dve.wait_ge(sil_ready, n + 1)
                dve.wait_ge(c_ready, m + 1)
                V.tensor_tensor(hid[:, j % 4, :], ps_s[:, j % 2, 1, :], hid[:, j % 4, :], ALU.mult).then_inc(hid_ready, 1)
                dve.wait_ge(hid_ready, m + 1)
                dve.wait_ge(y_done, n - 3)
                V.tensor_copy(hid_hi[:, j % 4, :], hid[:, j % 4, :]).then_inc(high_routed, 1)

            def keep_gate(tc):
                dve.wait_ge(gate_turned, tc + 1)
                V.tensor_copy(gate[:, bass.ts(tc, 4), :], ps_y[:, bass.ts(tc, 512)].rearrange("p (t d) -> p t d", t=4))\
                    .then_inc(gate_done, 1)

            for j in range(NBR):
                weigh(j, SHARED + j)
            dve.wait_ge(ld_pos, 3 * DMA)
            dve.wait_ge(wvall_ready, 1)
            link(V.tensor_scalar(wmax[:, 2:3], wmax[:, 1:2], 2.0 ** -100, None, ALU.max))
            link(V.tensor_single_scalar(wmax[:, 2:3].bitcast(U32), wmax[:, 2:3].bitcast(U32), 0x7F800000, ALU.bitwise_and))
            link(V.reciprocal(wmax[:, 3:4], wmax[:, 2:3]))
            split_weights(0)

            def routed_chunk(t):
                for j in range(NBR):
                    weigh(j, t * NBR + (SHARED + NBR + j))
                    if j == 7:
                        keep_gate(t)
                    if isinstance(t, int) and j % 2 == 1:
                        aux(PRE[j // 2], j // 2, 0, 0, True, 0)
                        if j % 4 == 3:
                            rope_add(j // 4)

            with dve.Fori(0, NQ - 2) as t:
                routed_chunk(t)
            routed_chunk(NQ - 2)
            keep_gate(NQ - 1)

            dve.wait_ge(gate_done, 4)

            def combine_max(U, g, k):
                dve.wait_ge(aux_free, k)
                V.tensor_reduce(max_n[:, U % 2, :], max_p[:, U % 2, :, :], AX.X, ALU.max, negate=True).then_inc(max_ready, 1)

            def low_probs(L, g):
                dve.wait_ge(probs_ready, L + 1 + PAIR_STEPS * g)
                c = slice(0, dve_low(L))
                V.tensor_tensor(pl[:, L % 4, c], pf[:, L % PF, c], ph[:, L % 4, c], ALU.subtract).then_inc(pl_dve, 1)

            def take_rec(U, g):
                dve.wait_ge(acc_copied, U + UNITS * g)
                V.reciprocal(o_rec[:, (U - 1) % 2, :], o_raw[:, (U - 1) % 2, :, DH]).then_inc(rec_ready, 1)

            def unit(U, g, k, last):
                hd = U // NQ
                hn = hd + 1 + 2 * g
                for s in range(STEPS):
                    L = U * STEPS + s
                    sl = STEPS * (U % NQ) + s
                    if s == MAX_AT and not (last and U + 1 >= UNITS):
                        combine_max(U + 1, g, k + AP * g)
                    Ln = L + LEAD - 1
                    work = items(U, s, last)
                    for n, it in enumerate(work):
                        aux(it, k, g, hn, False, 1 - hd % 2)
                        k += 1
                        if n == 0 and not (last and Ln >= PAIR_STEPS):
                            low_probs(Ln, g)
                    if not work and not (last and Ln >= PAIR_STEPS):
                        low_probs(Ln, g)
                    if s == 1 and not (isinstance(g, int) and U + UNITS * g == 0):
                        take_rec(U, g)
                    if sl == SPLIT_AT and not last:
                        split_weights(hn + 1)
                    if last and NQ < U < UNITS - 1 and s == STEPS - 1:
                        finish(U - 1 - NQ, k + AP * g)
                return k

            def finish(c, k):
                dve.wait_ge(ld_again, DMA)
                dve.wait_ge(aux_free, k)
                t = slice(QT * c, QT * c + QT)
                link(V.scalar_tensor_tensor(out=s_acc[:, t, :], in0=s_acc[:, t, :], scalar=wmax[:, 2:3],
                                            in1=bout_sb[:].unsqueeze(1).to_broadcast([P, QT, D]),
                                            op0=ALU.mult, op1=ALU.add))
                link(V.tensor_tensor(s_acc[:, t, :], s_acc[:, t, :], gate[:, t, :], ALU.mult))
                V.tensor_tensor(o_sb[:, t, :], s_acc[:, t, :], x_again[:, t, :], ALU.add).then_inc(fin, 1)

            for k in range(8, len(PRE)):
                aux(PRE[k], k, 0, 0, True, 0)
                if PRE[k] == ("v", NV - 1):
                    link(V.memset(s_acc[:], 0.0))
                if PRE[k] == ("max", 0, QT - 1, KC - 1):
                    combine_max(0, 0, k + 1)
                if k == FIRST + 5:
                    low_probs(0, 0)
            low_probs(1, 0)
            split_weights(1)
            k = len(PRE)
            k = unit(0, 0, k, False)
            with dve.Fori(0, PAIRS - 1) as g:
                kk = k
                for U in range(1, UNITS + 1):
                    kk = unit(U, g, kk, False)
            for U in range(1, UNITS):
                k = unit(U, PAIRS - 1, k, True)
            take_rec(UNITS, PAIRS - 1)
            finish(NQ - 2, k + AP * (PAIRS - 1))
            for it in (("turn_o", NQ - 1), ("out_proj", NQ - 1)):
                aux(it, k, PAIRS - 1, 0, False, 0)
                k += 1
            finish(NQ - 1, k + AP * (PAIRS - 1))

        @block.gpsimd
        def _(pool):
            G = nc.gpsimd
            pool.wait_ge(mlp_high, 2)
            G.tensor_tensor(w2_lo[:], w2_sb[:], w2_hi[:].bitcast(F32), ALU.subtract).then_inc(w2_split, 1)

            def low_hidden(j):
                G.tensor_tensor(hid_lo[:, j % 4, :], hid[:, j % 4, :], hid_hi[:, j % 4, :].bitcast(F32), ALU.subtract)\
                    .then_inc(low_ready, 1)

            pool.wait_ge(w2_split, 1)
            with pool.Fori(0, NQ) as t:
                for i in range(NBS):
                    pool.wait_ge(high_shared, t * NBS + (i + 1))
                    low_hidden(i)
            pool.wait_ge(wmax_ready, 1)
            G.partition_all_reduce(wmax[:, 1:2], wmax[:, 0:1], P, RMAX).then_inc(wvall_ready, 1)
            pool.wait_ge(wvall_ready, 1)
            def low_part(c, hn):
                pool.wait_ge(hi_done, 4 * hn + c + 1)
                G.tensor_tensor(qk_lo[:, c * 512:(c + 1) * 512], turn1[:, c % 2, :],
                                qk_hi[:, c * 512:(c + 1) * 512].bitcast(F32), ALU.subtract).then_inc(lo_done, 1)

            with pool.Fori(0, NQ - 1) as t:
                for j in range(NBR):
                    pool.wait_ge(high_routed, t * NBR + (j + 1))
                    low_hidden(j)
            for j in range(NBR):
                pool.wait_ge(high_routed, (NQ - 1) * NBR + j + 1)
                low_hidden(j)
                if j in (6, 10, 14):
                    low_part(j // 4 - 1, 0)
            low_part(3, 0)
            pool.wait_ge(lo_done, 4)
            pool.wait_ge(gate_done, 4)
            for a in range(2):
                G.memset(km2[a][DH:DH + 2, :].bitcast(F32), 1.0).then_inc(const_ready, 1)
                pool.wait_ge(const_ready, 2 * a + 1)
                G.memset(v_sb[a][:, :, DH:DH + 1], 1.0).then_inc(const_ready, 1)
                pool.wait_ge(const_ready, 2 * a + 2)

            def rope_add(c, hn, k):
                pool.wait_ge(aux_free, k)
                G.tensor_tensor(turn2[:, c % 2, :], turn2[:, c % 2, :], fenc[:, c * 512:(c + 1) * 512], ALU.add).then_inc(rope_a, 1)
                pool.wait_ge(rope_a, 4 * hn + c + 1)
                G.tensor_tensor(turn1[:, c % 2, :], turn1[:, c % 2, :], turn2[:, c % 2, :], ALU.add).then_inc(rope_sum, 1)

            def low_probs(L, g):
                pool.wait_ge(probs_ready, L + 1 + PAIR_STEPS * g)
                c = slice(dve_low(L), 2 * QC)
                G.tensor_tensor(pl[:, L % 4, c], pf[:, L % PF, c], ph[:, L % 4, c], ALU.subtract).then_inc(pl_pool, 1)

            def add_parts(U, g):
                pool.wait_ge(acc_copied, U + UNITS * g)
                r = o_raw[:, (U - 1) % 2, :, :]
                G.tensor_tensor(o_sum[:], r[:, :, 0:DH], r[:, :, DH + 1:OW], ALU.add).then_inc(osum_ready, 1)

            def normalise(U, g):
                pool.wait_ge(rec_ready, U + UNITS * g)
                pool.wait_ge(osum_ready, U + UNITS * g)
                qc, a = (U - 1) % NQ, ((U - 1) // NQ) % 2
                G.tensor_tensor(o_sb[:, QT * qc:QT * qc + QT, a * DH:(a + 1) * DH], o_sum[:],
                                o_rec[:, (U - 1) % 2, :].unsqueeze(2).to_broadcast([P, QT, DH]), ALU.mult).then_inc(o_ready, 1)

            def unit(U, g, k, last):
                hd = U // NQ
                hn = hd + 1 + 2 * g
                prep = not (last and hd % 2 == 1)
                rot_k = 0
                for s in range(STEPS):
                    L = U * STEPS + s
                    sl = STEPS * (U % NQ) + s
                    post = not (isinstance(g, int) and U + UNITS * g == 0)
                    if not (last and L + LEAD - 1 >= PAIR_STEPS):
                        low_probs(L + LEAD - 1, g)
                    for it in items(U, s, last):
                        k += 1
                        if it[0] == "rot":
                            rot_k = k + AP * g
                    if prep and sl - 1 in ROT_AT:
                        rope_add(ROT_AT.index(sl - 1), hn, rot_k)
                    if prep and sl - 3 in ROT_AT:
                        low_part(ROT_AT.index(sl - 3), hn)
                    if s == 1 and post:
                        add_parts(U, g)
                    if s == 2 and post:
                        normalise(U, g)
                return k

            k = len(PRE)
            for L in range(LEAD - 1):
                low_probs(L, 0)
            k = unit(0, 0, k, False)
            with pool.Fori(0, PAIRS - 1) as g:
                kk = k
                for U in range(1, UNITS + 1):
                    kk = unit(U, g, kk, False)
            for U in range(1, UNITS):
                k = unit(U, PAIRS - 1, k, True)
            add_parts(UNITS, PAIRS - 1)
            normalise(UNITS, PAIRS - 1)


def constants():
    freqs = (10000.0 ** (-np.arange(0, DH, 2, dtype=np.float64) / DH)).astype(np.float32)
    pos = np.arange(N, dtype=np.float32)[:, None]
    ang = (pos * freqs).astype(np.float64)
    cos = np.repeat(np.cos(ang), 2, axis=1).T.astype(np.float32)
    sin = np.repeat(np.sin(ang), 2, axis=1).T.astype(np.float32)
    sin[:DH // 2] *= -1
    ff = (pos * np.arange(1, 17, dtype=np.float32)).astype(np.float64)
    four = np.concatenate([np.sin(ff), np.cos(ff)], axis=1).T.astype(np.float32)
    expand = np.zeros((P, NBR, P), np.float32)
    for j in range(NBR):
        for c in range(P):
            expand[4 * j + c // 32, j, c] = expand[E + 4 * j + c // 32, j, c] = 1
    return {"cos": np.concatenate([cos, cos]), "sin": np.concatenate([sin, sin]), "four": four,
            "expand": expand, "eye": np.eye(P, dtype=np.float32)}


def kernel(**inputs):
    import numpy as _np
    import concourse.bacc as _bacc
    from concourse import mybir as _mybir
    from concourse.bass_utils import run_bass_kernel_spmd as _run

    i = {k.removeprefix("L0_"): _np.asarray(v) for k, v in inputs.items()}
    swap = _np.concatenate([_np.arange(1, DH, 2), _np.arange(0, DH, 2)])
    w = i["attn_w_qkv"].reshape(3, H, DH, D)
    w_head = _np.concatenate([w[0], w[1], w[0][:, swap], w[1][:, swap], w[2]], axis=1).transpose(0, 2, 1)
    w1 = _np.concatenate([i["ffn_w1"].transpose(1, 0, 2).reshape(D, -1), i["ffn_sw1"].transpose(1, 0, 2).reshape(D, -1)], axis=1)
    b1 = _np.concatenate([i["ffn_b1"].reshape(-1), i["ffn_sb1"].reshape(-1)]).reshape(NB, P).T
    w2 = _np.concatenate([i["ffn_w2"].reshape(-1, D), i["ffn_sw2"].reshape(-1, D)]).reshape(NB, P, D).transpose(1, 0, 2).reshape(P, HID)
    wf = i["attn_w_fproj"].T
    bf = i["attn_b_fproj"][:, None]
    c = constants()
    arrays = {
        "x": i["attn_x"], "w_head": w_head, "wqkv_all": i["attn_w_qkv"].reshape(P, -1),
        "wf": _np.concatenate([wf, wf], axis=1), "bf": _np.concatenate([bf, bf]), "four": c["four"],
        "cos": c["cos"], "sin": c["sin"], "w_out": i["attn_w_out"].T.reshape(PAIRS, P, D),
        "b_out": _np.tile(i["attn_b_out"], (P, 1)), "rw": i["ffn_router_w"],
        "rb": _np.tile(i["ffn_router_b"], (P, 1)), "w1": w1, "b1": b1, "w2": w2,
        "b2": _np.concatenate([i["ffn_b2"], i["ffn_b2"]]), "sb2": i["ffn_sb2"].T, "expand": c["expand"], "eye": c["eye"],
    }
    arrays = {k: _np.ascontiguousarray(v) for k, v in arrays.items()}
    nc = _bacc.Bacc("TRN2", target_bir_lowering=False, num_devices=1)
    args = [nc.dram_tensor(k, v.shape, _mybir.dt.from_np(v.dtype), kind="ExternalInput").ap() for k, v in arrays.items()]
    args.append(nc.dram_tensor("out", (1, N, D), _mybir.dt.float32, kind="ExternalOutput").ap())
    program(nc, *args)
    r = _run(nc, [arrays], core_ids=[0])
    return r.results[0]["out"]
```
